# Optimizing a Trainium2 kernel written in Bass

```python
import numpy as np
import jax
import jax.numpy as jnp

def _softmax(x, axis=-1):
    return jax.nn.softmax(x, axis=axis)
def _gelu(x):
    return jax.nn.gelu(x, approximate=True)
def _silu(x):
    return jax.nn.silu(x)
def _sigmoid(x):
    return jax.nn.sigmoid(x)
def _layernorm(x, axis=-1, eps=1e-5):
    m = jnp.mean(x, axis=axis, keepdims=True)
    v = jnp.var(x, axis=axis, keepdims=True)
    return (x - m) / jnp.sqrt(v + eps)
def _scatter_add(tgt, idx, src, axis=0):
    return tgt.at[idx].add(src)
def _segment_sum(src, seg, n):
    return jax.ops.segment_sum(src, seg, n)

kernel_name = 'mk_metaformer_d1_conv_nhwc256_2a6b09'

def setup_inputs(seed: int = 0):
    np.random.seed(seed)
    _w = jnp.asarray
    def _rec_inputs():
        import jax
        import jax.numpy as jnp
        _gk = jax.random.key(seed)
        x = -0.0005153 + 1.001 * jax.random.normal(jax.random.fold_in(_gk, 1), (4, 56, 56, 256), jnp.float32)
        return x
    x = _rec_inputs()
    def _L0_conv_setup():
        import jax, jax.numpy as jnp
        import numpy as np
        EMBED = 256
        HEADS = 8
        HEAD_DIM = EMBED // HEADS
        K = 7
        DIL = 1
        PAD = DIL * (K - 1) // 2
        B, H, W = (4, 56, 56)

        def _unfold(t):
            h, w = (t.shape[2], t.shape[3])
            tp = jnp.pad(t, ((0, 0), (0, 0), (PAD, PAD), (PAD, PAD)))
            patches = [tp[:, :, i * DIL:i * DIL + h, j * DIL:j * DIL + w] for i in range(K) for j in range(K)]
            return jnp.stack(patches, axis=2)
        key = jax.random.key(seed)
        ks = jax.random.split(key, 9)
        d = {'x': jax.random.normal(ks[0], (B, H, W, EMBED), jnp.float32)}
        for i, name in enumerate(['wq', 'wk', 'wv', 'wo']):
            d[name] = jax.random.normal(ks[1 + i], (EMBED, EMBED), jnp.float32) * 0.02
        for i, name in enumerate(['bq', 'bk', 'bv', 'bo']):
            d[name] = jax.random.normal(ks[5 + i], (EMBED,), jnp.float32) * 0.02
        return d
    _L0_conv_all = _L0_conv_setup()
    _L0_conv_in = {k: v for k, v in _L0_conv_all.items() if k in ('wq', 'bq', 'wk', 'bk', 'wv', 'bv', 'wo', 'bo', )}
    del _L0_conv_all

    def _L0_ffn_setup():
        import jax, jax.numpy as jnp
        import numpy as np
        B, T, D, H, E = (16, 4096, 256, 512, 8)
        key = jax.random.key(seed)
        ks = jax.random.split(key, 5)
        x = jax.random.normal(ks[0], (B, T, D), dtype=jnp.float32)
        gate_w = jax.random.normal(ks[1], (D, E), dtype=jnp.float32) * 0.02
        gate_b = jnp.zeros((E,), dtype=jnp.float32)
        W1 = jax.random.normal(ks[2], (E, D, H), dtype=jnp.float32) * 0.02
        b1 = jnp.zeros((E, H), dtype=jnp.float32)
        W2 = jax.random.normal(ks[3], (E, H, D), dtype=jnp.float32) * 0.02
        b2 = jnp.zeros((E, D), dtype=jnp.float32)
        return {'x': x, 'gate_w': gate_w, 'gate_b': gate_b, 'W1': W1, 'b1': b1, 'W2': W2, 'b2': b2}
    _L0_ffn_all = _L0_ffn_setup()
    _L0_ffn_in = {k: v for k, v in _L0_ffn_all.items() if k in ('gate_w', 'gate_b', 'W1', 'b1', 'W2', 'b2', )}
    del _L0_ffn_all

    return {
        "x": x,
        "L0_conv_wq": _L0_conv_in["wq"],
        "L0_conv_bq": _L0_conv_in["bq"],
        "L0_conv_wk": _L0_conv_in["wk"],
        "L0_conv_bk": _L0_conv_in["bk"],
        "L0_conv_wv": _L0_conv_in["wv"],
        "L0_conv_bv": _L0_conv_in["bv"],
        "L0_conv_wo": _L0_conv_in["wo"],
        "L0_conv_bo": _L0_conv_in["bo"],
        "L0_ffn_gate_w": _L0_ffn_in["gate_w"],
        "L0_ffn_gate_b": _L0_ffn_in["gate_b"],
        "L0_ffn_W1": _L0_ffn_in["W1"],
        "L0_ffn_b1": _L0_ffn_in["b1"],
        "L0_ffn_W2": _L0_ffn_in["W2"],
        "L0_ffn_b2": _L0_ffn_in["b2"],
    }

def reference(x, L0_conv_wq, L0_conv_bq, L0_conv_wk, L0_conv_bk, L0_conv_wv, L0_conv_bv, L0_conv_wo, L0_conv_bo, L0_ffn_gate_w, L0_ffn_gate_b, L0_ffn_W1, L0_ffn_b1, L0_ffn_W2, L0_ffn_b2):
    import jax
    import jax.numpy as jnp
    def _L0_conv_ref(x, wq, bq, wk, bk, wv, bv, wo, bo):
        import jax, jax.numpy as jnp
        import numpy as np
        EMBED = 256
        HEADS = 8
        HEAD_DIM = EMBED // HEADS
        K = 7
        DIL = 1
        PAD = DIL * (K - 1) // 2
        B, H, W = (4, 56, 56)

        def _unfold(t):
            h, w = (t.shape[2], t.shape[3])
            tp = jnp.pad(t, ((0, 0), (0, 0), (PAD, PAD), (PAD, PAD)))
            patches = [tp[:, :, i * DIL:i * DIL + h, j * DIL:j * DIL + w] for i in range(K) for j in range(K)]
            return jnp.stack(patches, axis=2)
        b, h, w, c = x.shape
        scale = HEAD_DIM ** (-0.5)
        q = x @ wq.T + bq
        k = x @ wk.T + bk
        v = x @ wv.T + bv

        def to_nh(t):
            return t.reshape(b, h, w, HEADS, HEAD_DIM).transpose(0, 3, 4, 1, 2).reshape(b * HEADS, HEAD_DIM, h, w)
        q, k, v = (to_nh(q), to_nh(k), to_nh(v))
        k_unf = _unfold(k)
        v_unf = _unfold(v)
        logits = jnp.einsum('ndhw,ndkhw->nkhw', q, k_unf) * scale
        attn = jax.nn.softmax(logits, axis=1)
        out = jnp.einsum('nkhw,ndkhw->ndhw', attn, v_unf)
        out = out.reshape(b, HEADS, HEAD_DIM, h, w).transpose(0, 3, 4, 1, 2).reshape(b, h, w, c)
        return out @ wo.T + bo

    def _L0_ffn_ref(x, gate_w, gate_b, W1, b1, W2, b2):
        import jax, jax.numpy as jnp
        import numpy as np
        B, T, D, H, E = (16, 4096, 256, 512, 8)
        Bb, Tt, Dd = x.shape
        Ee = gate_w.shape[1]
        xf = x.reshape(-1, Dd)
        N = xf.shape[0]
        logits = xf @ gate_w + gate_b
        probs = jax.nn.softmax(logits, axis=-1)
        top2_vals, top2_idx = jax.lax.top_k(probs, 2)
        cw = jnp.zeros((N, Ee), dtype=xf.dtype).at[jnp.arange(N)[:, None], top2_idx].add(top2_vals)

        def step(acc, params):
            w1, bb1, w2, bb2, we = params
            h = jax.nn.gelu(xf @ w1 + bb1, approximate=False)
            y = h @ w2 + bb2
            return (acc + we[:, None] * y, None)
        out, _ = jax.lax.scan(step, jnp.zeros_like(xf), (W1, b1, W2, b2, cw.T))
        return out.reshape(Bb, Tt, Dd)

    def _gn(v, G=32, eps=1e-5):
        B_, H_, W_, C_ = v.shape
        g = v.reshape(B_, H_, W_, G, C_ // G)
        m = jnp.mean(g, axis=(1, 2, 4), keepdims=True)
        s = jnp.var(g, axis=(1, 2, 4), keepdims=True)
        return ((g - m) / jnp.sqrt(s + eps)).reshape(v.shape)

    def _ln_c(v, eps=1e-6):
        m = jnp.mean(v, axis=-1, keepdims=True)
        s = jnp.var(v, axis=-1, keepdims=True)
        return (v - m) / jnp.sqrt(s + eps)

    def _ln_t(v, eps=1e-5):
        m = jnp.mean(v, axis=-1, keepdims=True)
        s = jnp.var(v, axis=-1, keepdims=True)
        return (v - m) / jnp.sqrt(s + eps)

    def _to_tokens(v):
        B_, H_, W_, C_ = v.shape
        return v.reshape(B_, H_ * W_, C_)
    def _from_tokens(t, like):
        return t.reshape(like.shape)

    x = x + _L0_conv_ref(_ln_c(x), L0_conv_wq, L0_conv_bq, L0_conv_wk, L0_conv_bk, L0_conv_wv, L0_conv_bv, L0_conv_wo, L0_conv_bo)
    t = _to_tokens(x)
    t = t + _L0_ffn_ref(_ln_t(t), L0_ffn_gate_w, L0_ffn_gate_b, L0_ffn_W1, L0_ffn_b1, L0_ffn_W2, L0_ffn_b2)
    x = _from_tokens(t, x)
    return x


_drawn_inputs = setup_inputs


def setup_inputs(seed=0):
    import zlib

    import numpy as np

    out = dict(_drawn_inputs(seed))
    spreads = {'L0_ffn_gate_b': (0.0, 0.425), 'L0_ffn_b1': (0.0, 0.8), 'L0_ffn_b2': (0.0, 0.312)}
    factors = {'L0_conv_wq': 8.0,
     'L0_conv_bq': 8.0,
     'L0_conv_wk': 8.0,
     'L0_conv_bk': 195.82,
     'L0_conv_wv': 3.858,
     'L0_conv_bv': 8.0,
     'L0_conv_wo': 3.563,
     'L0_conv_bo': 2.898,
     'L0_ffn_W1': 2.85,
     'L0_ffn_W2': 2.676}
    for name, (base, spread) in spreads.items():
        noise = np.random.default_rng([zlib.crc32(name.encode()), seed]).standard_normal(out[name].shape)
        drawn = base * np.exp(spread * noise) if base else spread * noise
        out[name] = jnp.asarray(drawn.astype(out[name].dtype))
    for name, factor in factors.items():
        out[name] = (out[name] * factor).astype(out[name].dtype)
    return out
```

```python
from contextlib import ExitStack

import concourse.bass as bass
from concourse import mybir

ALU = mybir.AluOpType
ACT = mybir.ActivationFunctionType
AX = mybir.AxisListType
F32 = mybir.dt.float32

WIN = 7
HALO = WIN // 2
HEADS = 8
ROWS = 4
QS = 4
KS = QS + WIN - 1
KK = KS * KS
QQ = QS * QS
P = 128
TB = [4, 4, 3, 3]
T0 = [0, 4, 8, 11]
NEG = -1.0e30


class Band:

    def __init__(self, m, c, total, per_image):
        self.m, self.c, self.total, self.per_image = m, c, total, per_image
        self.static = isinstance(m, int)

    def at(self, d):
        return Band(self.m, self.c + d, self.total, self.per_image)

    @property
    def inside(self):
        return not self.static or 0 <= 2 * self.m + self.c < self.total

    @property
    def parity(self):
        return self.c % 2

    def lin(self, a, b=0):
        return self.m * (2 * a) + (a * self.c + b)

    def turn(self, a, b=0):
        return (self.m + self.c // 2) * a + b

    def row(self):
        return self.lin(ROWS) + ((self.m + self.c // 2) // (self.per_image // 2)) * HALO

    def key_row(self):
        pair = self.m + self.c // 2
        return ((pair % self.per_image) * 2 + self.c % 2) * ROWS + (pair // (self.per_image // 2)) % 2 * HALO


def build(nc, x, wqT, wkT, wvT, woT, bq, bk, bv, bo, gate_w, gate_b, mask, own, ident, pref, W1, b1, W2, b2, out):
    NIMG, H, W, C = x.shape
    NTOK = NIMG * H * W
    NB = H // ROWS
    NBANDS = NIMG * NB
    BT = ROWS * W
    HT = BT // 2
    NT = W // QS
    PW = W + HALO
    PROWS = NIMG * (H + HALO) + HALO
    FLAT = (PROWS + 1) * PW
    KIMG = min(NIMG, 2)
    KROWS = KIMG * (H + HALO) + HALO
    KFLAT = (KROWS + 1) * PW
    G = C // P
    HG = HEADS // G
    D = C // HEADS
    E = gate_w.shape[1]
    SCALE = float(D) ** -0.5
    assert sum(TB) == NT and NB % 2 == 0 and D == 32 and HT <= P

    with ExitStack() as ctx:
        def sb(name, shape, dt=F32):
            return ctx.enter_context(nc.sbuf_tensor(name, shape, dt))

        totals = {}

        def sem(name, total=None):
            s = ctx.enter_context(nc.semaphore(name))
            if total is not None:
                totals[id(s)] = total
            return s

        v_pad = nc.dram_tensor("v_pad", [FLAT, C], F32).ap()
        xn2_dram = nc.dram_tensor("xn2_dram", [NTOK, C], F32).ap()
        x_tok = x.rearrange("n h w c -> (n h w) c")
        x1_dram = out.rearrange("n h w c -> (n h w) c")

        HID = W1.shape[2]
        HC = HID // P
        logit = sb("logit", [P, 2 * NBANDS, E])
        cw = sb("cw", [P, 2 * NBANDS, E])
        b1_sb = sb("b1_sb", [P, E, HC])
        b2_sb = sb("b2_sb", [E, C])
        pref_sb = sb("pref_sb", [P, 1, E])
        id_sb = sb("id_sb", [P, P])
        early = ExitStack()
        keep_sb = sb

        def sb(name, shape, dt=F32):
            return early.enter_context(nc.sbuf_tensor(name, shape, dt))

        def psum(name, shape):
            return early.enter_context(nc.psum_tensor(name, shape, F32))

        wq_sb = sb("wq_sb", [P, G, C])
        wk_sb = sb("wk_sb", [P, G, C])
        wv_sb = sb("wv_sb", [P, G, C])
        wo_sb = sb("wo_sb", [P, G, C])
        gw_sb = sb("gw_sb", [P, G, E])
        bq_sb = sb("bq_sb", [P, G])
        bk_sb = sb("bk_sb", [P, G])
        bv_sb = sb("bv_sb", [P, 1, C])
        bo_sb = sb("bo_sb", [P, 1, C])
        gb_sb = sb("gb_sb", [P, 1, E])
        mask_sb = sb("mask_sb", [P, 1, KK])
        own_sb = sb("own_sb", [P, HG])
        half_sb = sb("half_sb", [P, 2])
        zero_sb = sb("zero_sb", [P, 3 * C])

        k_pad = sb("k_pad", [P, G, KFLAT])
        x_in = sb("x_in", [P, 2, 2, C])
        st1 = sb("st1", [P, 2, 6])
        mv1 = sb("mv1", [P, 2, 2])
        ve1 = sb("ve1", [P, 2])
        rs1 = sb("rs1", [P, 2])
        xn = sb("xn", [P, 2, C])
        xnT = sb("xnT", [P, G, BT])
        q_sb = sb("q_sb", [P, 2, G, BT])
        q_bd = sb("q_bd", [P, 2, G, NT, HEADS, QQ])
        v_sb = sb("v_sb", [P, 2, 2, C])
        v_win = sb("v_win", [P, 2, NT, C])
        s_sb = sb("s_sb", [P, 4, 4, KK])
        mx = sb("mx", [P, 4, 4])
        sm = sb("sm", [P, 4, 4])
        rs = sb("rs", [P, 4, 4])
        pT = sb("pT", [P, 2, 4, P])
        oT = sb("oT", [P, 2, G * ROWS, W])
        x_res = sb("x_res", [P, 2, 2, C])
        x1_sb = sb("x1_sb", [P, 2, 2, C])
        st2 = sb("st2", [P, 2, 6])
        mv2 = sb("mv2", [P, 2, 2])
        ve2 = sb("ve2", [P, 2])
        rs2 = sb("rs2", [P, 2])
        xn2 = sb("xn2", [P, 2, 2, C])
        xn2T = sb("xn2T", [P, G, BT])

        ps_tr = psum("ps_tr", [P, G, 2, HT])
        ps_qk = psum("ps_qk", [P, G, BT])
        ps_vy = psum("ps_vy", [P, 2, C])
        ps_s = [psum(f"ps_s{i}", [P, 4, P]) for i in range(2)]
        ps_t = [psum(f"ps_t{i}", [P, 4, P]) for i in range(2)]
        ps_o = psum("ps_o", [P, HG, G * QS, 4 * QS])

        early.close()
        g_m = keep_sb("g_m", [P, 2 * NBANDS])
        g_eq = keep_sb("g_eq", [P, 2 * NBANDS, E])
        g_oh = keep_sb("g_oh", [P, 2 * NBANDS, E])
        g_p2 = keep_sb("g_p2", [P, 2 * NBANDS, E])
        w1_sb = keep_sb("w1_sb", [P, E, G, HID])
        w2_sb = keep_sb("w2_sb", [P, E, HC, C])
        f_x = keep_sb("f_x", [P, 2, 2, C])
        f_acc = keep_sb("f_acc", [P, 2, 2, C])
        f_xT = keep_sb("f_xT", [P, 2, G, BT])
        f_hT = keep_sb("f_hT", [P, 2, HC, BT])
        f_cw = keep_sb("f_cw", [P, 2, 2, E])
        f_cwT = keep_sb("f_cwT", [E, 2, HT])
        pf_tr = ctx.enter_context(nc.psum_tensor("pf_tr", [P, G, BT], F32))
        pf_h = [ctx.enter_context(nc.psum_tensor(f"pf_h{i}", [P, 2, BT], F32)) for i in range(2)]
        pf_y = [ctx.enter_context(nc.psum_tensor(f"pf_y{i}", [P, 2, C], F32)) for i in range(2)]
        pf_b = ctx.enter_context(nc.psum_tensor("pf_b", [P, 2, C], F32))
        pf_c = ctx.enter_context(nc.psum_tensor("pf_c", [E, 2, HT], F32))

        NBAT = 4 * NBANDS
        s_w = sem("weights_loaded")
        s_zero = sem("zeros_made")
        s_rows = sem("key_pad_rows_cleared")
        s_init = sem("buffers_cleared")
        s_vz = sem("v_pads_stored")
        xld = [sem(f"x_loaded{p}", 16 * NBANDS // 2) for p in range(2)]
        xrl = [sem(f"residual_loaded{p}", 16 * NBANDS // 2) for p in range(2)]
        vst = [sem(f"v_stored{p}", 64 * NBANDS // 2) for p in range(2)]
        vwl = [sem(f"v_window_loaded{p}", 16 * KS * NBANDS // 2) for p in range(2)]
        x1st = [sem(f"x1_stored{p}", 16 * NBANDS // 2) for p in range(2)]
        xnst = [sem(f"xn2_stored{p}", 16 * NBANDS // 2) for p in range(2)]
        qk = sem("scores_made", NBAT)
        msa = sem("scores_masked", NBAT)
        ms = sem("maxima_made", NBAT)
        sub = sem("maxima_subtracted", NBAT)
        exp = sem("exponentials_made", NBAT)
        sms = sem("sums_made", NBAT)
        rcp = sem("sums_inverted", NBAT)
        nrm = sem("probabilities_made", NBAT)
        tr = sem("probabilities_turned", NBAT)
        evt = sem("turned_probabilities_kept", NBAT)
        pv = sem("values_weighted", NBAT)
        exd = sem("heads_gathered_by_vector", NBAT)
        exa = sem("heads_gathered_by_scalar", NBAT)
        bst1 = sem("ln1_stats", 2 * NBANDS)
        agg1 = sem("ln1_moments", 2 * NBANDS)
        var1 = sem("ln1_variance", NBANDS)
        rsq1 = sem("ln1_scale", NBANDS)
        xn_done = sem("ln1_done", 2 * NBANDS)
        tx = sem("ln1_turned", NBANDS)
        txe = sem("ln1_turned_kept", NBANDS)
        pq = sem("q_made", NBANDS)
        qe = sem("q_kept", NBANDS)
        qbd = sem("q_spread", G * NBANDS)
        pvj = sem("v_made", NBANDS)
        ve = sem("v_kept", NBANDS)
        pk = sem("k_made", NBANDS)
        ke = sem("k_kept", NBANDS)
        yd = sem("attention_projected", NBANDS)
        xb = sem("residual_biased", NBANDS)
        x1 = sem("x1_made", NBANDS)
        bst2 = sem("ln2_stats", 2 * NBANDS)
        agg2 = sem("ln2_moments", 2 * NBANDS)
        var2 = sem("ln2_variance", NBANDS)
        rsq2 = sem("ln2_scale", NBANDS)
        xn2_done = sem("ln2_done", 2 * NBANDS)
        tx2 = sem("ln2_turned", NBANDS)
        tx2e = sem("ln2_turned_kept", NBANDS)
        lg = sem("logits_made", NBANDS)
        lge = sem("logits_kept", NBANDS)
        s_w12 = sem("expert_weights_loaded")
        gate = sem("gate_steps")
        gexp = sem("gate_exponentials")
        fxl = [sem(f"ffn_tokens_loaded{p}", 16 * NBANDS // 2) for p in range(2)]
        fal = [sem(f"ffn_residual_loaded{p}", 16 * NBANDS // 2) for p in range(2)]
        fst = [sem(f"ffn_stored{p}", 16 * NBANDS // 2) for p in range(2)]
        ftx = sem("ffn_turned", NBANDS)
        ftxe = sem("ffn_turned_kept", NBANDS)
        fcw = sem("ffn_weights_picked", NBANDS)
        fct = sem("ffn_weights_turned", NBANDS)
        fcte = sem("ffn_weights_turned_kept", NBANDS)
        fb = sem("ffn_bias_made", NBANDS)
        fbd = sem("ffn_bias_added", NBANDS)
        fh = sem("ffn_hidden_made", 2 * E * NBANDS)
        fg = sem("ffn_gelu_made", 2 * E * NBANDS)
        fy = sem("ffn_out_made", E * NBANDS)
        fa = sem("ffn_out_added", 2 * E * NBANDS)

        def due(s, value, alone=None):
            if isinstance(value, int):
                value = min(value, totals.get(id(s), value))
                return [value] if value > 0 else []
            if alone is not None:
                value = alone.lower_val(value)
                alone.wait_ge(s_zero, 1)
            return [value]

        first_loop, last_loop = 2, (NBANDS - 4) // 2
        LEAD, LAG = 4, 3

        def run(e, body):
            for c in range(-LEAD, 2 * first_loop):
                body(Band(0, c, NBANDS, NB))
            with e.Fori(first_loop, last_loop) as m:
                for c in range(2):
                    body(Band(m, c, NBANDS, NB))
            for c in range(2 * last_loop, NBANDS + LAG):
                body(Band(0, c, NBANDS, NB))

        def lag(j, k, d):
            n = k - d
            return j.at(n // 4), n % 4

        block = ctx.enter_context(nc.Block())

        @block.sync
        def _(sp):
            for dst, src in ((wq_sb, wqT), (wk_sb, wkT), (wv_sb, wvT), (wo_sb, woT), (gw_sb, gate_w)):
                sp.dma_start(dst[:], src.rearrange("(g p) n -> p g n", p=P)).then_inc(s_w, 16)
            for dst, src in ((bq_sb, bq), (bk_sb, bk)):
                sp.dma_start(dst[:], src).then_inc(s_w, 16)
            for dst, src, n in ((bv_sb, bv, C), (bo_sb, bo, C), (gb_sb, gate_b, E)):
                sp.dma_start(dst[:, 0], bass.AP(src.tensor, 0, [[0, P], [1, n]])).then_inc(s_w, 16)
            sp.dma_start(mask_sb[:, 0], mask).then_inc(s_w, 16)
            sp.dma_start(pref_sb[:, 0], bass.AP(pref.tensor, 0, [[0, P], [1, E]])).then_inc(s_w, 16)
            sp.dma_start(own_sb[:], own).then_inc(s_w, 16)
            sp.dma_start(id_sb[:], ident).then_inc(s_w, 16)
            for count in due(s_zero, 1, sp):
                sp.wait_ge(s_zero, count)
            vt = v_pad.tensor
            n0 = PROWS // 2
            sp.dma_start(bass.AP(vt, 0, [[PW * C, n0], [1, HALO * C]]), zero_sb[0:n0, :]).then_inc(s_vz, 16)
            sp.dma_start(bass.AP(vt, n0 * PW * C, [[PW * C, PROWS + 1 - n0], [1, HALO * C]]),
                         zero_sb[0:PROWS + 1 - n0, :]).then_inc(s_vz, 16)
            for count in due(s_vz, 32, sp):
                sp.wait_ge(s_vz, count)
            for n in range(NIMG + 1):
                sp.dma_start(bass.AP(vt, n * (H + HALO) * PW * C, [[HALO * C, PW], [1, HALO * C]]),
                             zero_sb[0:PW, :]).then_inc(s_vz, 16)
            n_vz = 16 * (2 + NIMG + 1)

            def band_tokens(t, at):
                return bass.AP(t.tensor, at, [[C, HT], [HT * C, 2], [1, C]])

            def body(j):
                b = j.at(4)
                if b.inside:
                    for count in due(xn_done, j.at(4).lin(2, -2), sp):
                        sp.wait_ge(xn_done, count)
                    sp.dma_start(x_in[0:HT, b.parity], band_tokens(x_tok, j.at(4).lin(BT * C))).then_inc(xld[b.parity], 16)
                if j.inside:
                    for count in due(x1, j.lin(1, -1), sp):
                        sp.wait_ge(x1, count)
                    sp.dma_start(x_res[0:HT, j.parity], band_tokens(x_tok, j.lin(BT * C))).then_inc(xrl[j.parity], 16)
                b = j.at(-2)
                if b.inside:
                    for count in due(x1, b.lin(1, 1), sp):
                        sp.wait_ge(x1, count)
                    sp.dma_start(band_tokens(x1_dram, b.lin(BT * C)), x1_sb[0:HT, b.parity]).then_inc(x1st[b.parity], 16)
                b = j.at(2)
                if b.inside:
                    for count in due(ve, b.lin(1, 1), sp):
                        sp.wait_ge(ve, count)
                    v_at = (b.row() + HALO) * (PW * C)
                    for h in range(2):
                        for r in range(2):
                            sp.dma_start(
                                bass.AP(v_pad.tensor, v_at + ((2 * h + r) * PW + HALO) * C, [[C, W], [1, C]]),
                                v_sb[r * W:(r + 1) * W, b.parity, h, :]).then_inc(vst[b.parity], 16)
                b = j.at(-2)
                if b.inside:
                    for count in due(xn2_done, b.lin(2, 2), sp):
                        sp.wait_ge(xn2_done, count)
                    sp.dma_start(band_tokens(xn2_dram, b.lin(BT * C)), xn2[0:HT, b.parity]).then_inc(xnst[b.parity], 16)
                b = j.at(1)
                if b.inside:
                    if j.static and j.c == -1:
                        for count in due(s_vz, n_vz, sp):
                            sp.wait_ge(s_vz, count)
                        for count in due(vst[0], 64, sp):
                            sp.wait_ge(vst[0], count)
                    for count in due(vst[j.parity], j.at(2).turn(64, 64), sp):
                        sp.wait_ge(vst[j.parity], count)
                    for count in due(pv, j.lin(4), sp):
                        sp.wait_ge(pv, count)
                    w_at = b.row() * (PW * C)
                    for r in range(KS):
                        sp.dma_start(v_win[KS * r:KS * r + KS, b.parity],
                                     bass.AP(v_pad.tensor, w_at + r * PW * C, [[C, KS], [QS * C, NT], [1, C]])
                                     ).then_inc(vwl[b.parity], 16)

            run(sp, body)
            for p in range(2):
                for count in due(x1st[p], totals[id(x1st[p])], sp):
                    sp.wait_ge(x1st[p], count)
                for count in due(xnst[p], totals[id(xnst[p])], sp):
                    sp.wait_ge(xnst[p], count)
            for s_, n in ((qk, NBAT), (pv, NBAT), (lge, NBANDS), (exd, NBAT), (exa, NBAT), (tx2e, NBANDS), (qbd, G * NBANDS)):
                for count in due(s_, n, sp):
                    sp.wait_ge(s_, count)
            for count in due(lg, NBANDS, sp):
                sp.wait_ge(lg, count)
            for e in range(E):
                sp.dma_start(w1_sb[:, e], W1[e].rearrange("(g p) n -> p g n", p=P)).then_inc(s_w12, 16)
                sp.dma_start(w2_sb[:, e], W2[e].rearrange("(g p) n -> p g n", p=P)).then_inc(s_w12, 16)
            sp.dma_start(b1_sb[:], b1).then_inc(s_w12, 16)
            sp.dma_start(b2_sb[:], b2).then_inc(s_w12, 16)

            def ffn(j):
                p = j.parity
                if j.inside:
                    for count in due(ftx, j.lin(1, -1), sp):
                        sp.wait_ge(ftx, count)
                    sp.dma_start(f_x[0:HT, p], band_tokens(xn2_dram, j.lin(BT * C))).then_inc(fxl[p], 16)
                    for count in due(fst[p], j.turn(16), sp):
                        sp.wait_ge(fst[p], count)
                    sp.dma_start(f_acc[0:HT, p], band_tokens(x1_dram, j.lin(BT * C))).then_inc(fal[p], 16)
                b = j.at(-1)
                if b.inside:
                    for count in due(fa, b.lin(2 * E, 2 * E), sp):
                        sp.wait_ge(fa, count)
                    sp.dma_start(band_tokens(x1_dram, b.lin(BT * C)), f_acc[0:HT, b.parity]).then_inc(fst[b.parity], 16)

            run(sp, ffn)
            for p in range(2):
                for count in due(fst[p], totals[id(fst[p])], sp):
                    sp.wait_ge(fst[p], count)

        @block.tensor
        def _(pe):
            for count in due(s_w, 16 * 14):
                pe.wait_ge(s_w, count)
            for count in due(s_init, 3):
                pe.wait_ge(s_init, count)

            def turn(src, dst):
                for h in range(2):
                    for g in range(G):
                        mm = pe.transpose(dst[:, g, h, :], src[0:HT, h, P * g:P * g + P], id_sb[0:HT, 0:HT])
                return mm

            def body(j):
                for k in range(4):
                    if j.inside:
                        if k == 0:
                            for count in due(qbd, j.lin(G, G)):
                                pe.wait_ge(qbd, count)
                            for count in due(ke, j.lin(1, 2)):
                                pe.wait_ge(ke, count)
                        for count in due(msa, j.lin(4, k - 1)):
                            pe.wait_ge(msa, count)
                        row = j.key_row() * PW
                        for t in range(TB[k]):
                            for g in range(G):
                                keys = bass.AP(k_pad[:].tensor, row + (g * KFLAT + QS * (T0[k] + t)),
                                               [[G * KFLAT, P], [PW, KS], [1, KS]])
                                qs = q_bd[:, j.parity, g, T0[k] + t].rearrange("p h q -> p (h q)")
                                mm = pe.matmul(ps_s[k % 2][:, t, 0:KK].rearrange("p (r c) -> p r c", r=KS),
                                               qs, keys, start=(g == 0), stop=(g == G - 1))
                        mm.then_inc(qk, 1)
                    b, kb = lag(j, k, 2)
                    if b.inside:
                        for count in due(nrm, b.lin(4, kb + 1)):
                            pe.wait_ge(nrm, count)
                        for count in due(evt, b.lin(4, kb - 1)):
                            pe.wait_ge(evt, count)
                        for t in range(TB[kb]):
                            mm = pe.transpose(ps_t[kb % 2][0:KK, t, :], s_sb[:, kb, t, :], id_sb[:, :])
                        mm.then_inc(tr, 1)
                    b, kb = lag(j, k, 3)
                    if b.inside:
                        for count in due(evt, b.lin(4, kb + 1)):
                            pe.wait_ge(evt, count)
                        for count in due(exd, b.lin(4, kb)):
                            pe.wait_ge(exd, count)
                        for count in due(exa, b.lin(4, kb)):
                            pe.wait_ge(exa, count)
                        if kb == 0:
                            for count in due(vwl[b.parity], b.turn(16 * KS, 16 * KS)):
                                pe.wait_ge(vwl[b.parity], count)
                        for t in range(TB[kb]):
                            for g in range(G):
                                dst = ps_o[:, :, QS * g:QS * g + QS, QS * t:QS * t + QS]
                                mm = pe.matmul(dst, v_win[0:KK, b.parity, T0[kb] + t, P * g:P * g + P],
                                               pT[0:KK, kb % 2, t, HG * QQ * g:HG * QQ * (g + 1)],
                                               start=True, stop=True)
                        mm.then_inc(pv, 1)
                    n, o = j.at(2), j.at(-2)
                    if k == 0 and n.inside:
                        for count in due(xn_done, n.lin(2, 2)):
                            pe.wait_ge(xn_done, count)
                        for count in due(tx2e, j.lin(1, -2)):
                            pe.wait_ge(tx2e, count)
                        turn(xn, ps_tr).then_inc(tx, 1)
                    if k == 1 and n.inside:
                        for count in due(txe, n.lin(1, 1)):
                            pe.wait_ge(txe, count)
                        for count in due(ke, n.lin(1)):
                            pe.wait_ge(ke, count)
                        for g in range(G):
                            for c in range(G):
                                dst = ps_qk[:, g, :].rearrange("p (t r c) -> p r t c", t=NT, r=QS)
                                mm = pe.matmul(dst, wq_sb[:, c, P * g:P * g + P], xnT[:, c, :],
                                               start=(c == 0), stop=(c == G - 1))
                        mm.then_inc(pq, 1)
                        for count in due(x1, j.lin(1, -1)):
                            pe.wait_ge(x1, count)
                        for h in range(2):
                            for c in range(G):
                                mm = pe.matmul(ps_vy[0:HT, h, :], xnT[:, c, HT * h:HT * h + HT], wv_sb[:, c, :],
                                               start=(c == 0), stop=(c == G - 1))
                        mm.then_inc(pvj, 1)
                    if k == 1 and o.inside:
                        for count in due(xn2_done, o.lin(2, 2)):
                            pe.wait_ge(xn2_done, count)
                        for count in due(txe, j.lin(1, 3)):
                            pe.wait_ge(txe, count)
                        turn(xn2[:, o.parity], ps_tr).then_inc(tx2, 1)
                    if k == 2 and n.inside:
                        for count in due(qe, n.lin(1, 1)):
                            pe.wait_ge(qe, count)
                        for g in range(G):
                            for c in range(G):
                                mm = pe.matmul(ps_qk[:, g, :], wk_sb[:, c, P * g:P * g + P], xnT[:, c, :],
                                               start=(c == 0), stop=(c == G - 1))
                        mm.then_inc(pk, 1)
                    if k == 2 and o.inside:
                        for count in due(tx2e, o.lin(1, 1)):
                            pe.wait_ge(tx2e, count)
                        for count in due(ve, j.lin(1, 3)):
                            pe.wait_ge(ve, count)
                        for h in range(2):
                            for c in range(G):
                                mm = pe.matmul(ps_vy[0:HT, h, 0:E], xn2T[:, c, HT * h:HT * h + HT], gw_sb[:, c, :],
                                               start=(c == 0), stop=(c == G - 1))
                        mm.then_inc(lg, 1)
                    b = j.at(-1)
                    if k == 3 and b.inside:
                        for count in due(exd, j.lin(4)):
                            pe.wait_ge(exd, count)
                        for count in due(exa, j.lin(4)):
                            pe.wait_ge(exa, count)
                        for count in due(lge, j.lin(1, -1)):
                            pe.wait_ge(lge, count)
                        for count in due(ve, j.lin(1, 3)):
                            pe.wait_ge(ve, count)
                        for h in range(2):
                            for g in range(G):
                                rows = slice(ROWS * g + 2 * h, ROWS * g + 2 * h + 2)
                                heads = oT[:, b.parity, rows, :].rearrange("p r c -> p (r c)")
                                mm = pe.matmul(ps_vy[0:HT, h, :], heads, wo_sb[:, g, :],
                                               start=(g == 0), stop=(g == G - 1))
                        mm.then_inc(yd, 1)

            run(pe, body)
            for count in due(s_w12, 16 * (2 * E + 2)):
                pe.wait_ge(s_w12, count)

            def ffn(j):
                n = j.at(1)
                p = j.parity

                def hidden(e):
                    for half in range(2):
                        for count in due(fg, j.lin(2 * E, 2 * e + half - 1)):
                            pe.wait_ge(fg, count)
                        for i in range(2):
                            hc = 2 * half + i
                            for c in range(G):
                                mm = pe.matmul(pf_h[half][:, i, :], w1_sb[:, e, c, P * hc:P * hc + P], f_xT[:, p, c, :],
                                               start=(c == 0), stop=(c == G - 1))
                        mm.then_inc(fh, 1)

                def outs(e):
                    for count in due(fg, j.lin(2 * E, 2 * e + 2)):
                        pe.wait_ge(fg, count)
                    for count in due(fa, j.lin(2 * E, 2 * (e - 1))):
                        pe.wait_ge(fa, count)
                    for h in range(2):
                        for hc in range(HC):
                            mm = pe.matmul(pf_y[e % 2][0:HT, h, :], f_hT[:, e % 2, hc, HT * h:HT * h + HT],
                                           w2_sb[:, e, hc, :], start=(hc == 0), stop=(hc == HC - 1))
                    mm.then_inc(fy, 1)

                if j.inside:
                    for count in due(ftxe, j.lin(1, 1)):
                        pe.wait_ge(ftxe, count)
                    hidden(0)
                if n.inside:
                    for count in due(fxl[n.parity], n.turn(16, 16)):
                        pe.wait_ge(fxl[n.parity], count)
                    for count in due(ftxe, j.lin(1, 1)):
                        pe.wait_ge(ftxe, count)
                    turn(f_x[:, n.parity], pf_tr[:].rearrange("p g (h t) -> p g h t", h=2)).then_inc(ftx, 1)
                if j.inside:
                    for count in due(fcw, j.lin(1, 1)):
                        pe.wait_ge(fcw, count)
                    for h in range(2):
                        mm = pe.transpose(pf_c[:, h, :], f_cw[0:HT, p, h, :], id_sb[0:HT, 0:HT])
                    mm.then_inc(fct, 1)
                    for e in range(1, E):
                        hidden(e)
                        outs(e - 1)
                        if e == 2:
                            for count in due(fcte, j.lin(1, 1)):
                                pe.wait_ge(fcte, count)
                            for count in due(fbd, j.lin(1)):
                                pe.wait_ge(fbd, count)
                            for h in range(2):
                                mm = pe.matmul(pf_b[0:HT, h, :], f_cwT[:, h, :], b2_sb[:], start=True, stop=True)
                            mm.then_inc(fb, 1)
                    outs(E - 1)

            run(pe, ffn)

        def gather_heads(e, copy, b, kb, hs, done):
            for count in due(pv, b.lin(4, kb + 1)):
                e.wait_ge(pv, count)
            if kb == 0:
                for count in due(yd, b.lin(1, -1)):
                    e.wait_ge(yd, count)
            n = TB[kb]
            for hh in hs:
                mm = copy(oT[D * hh:D * hh + D, b.parity, :, QS * T0[kb]:QS * (T0[kb] + n)],
                          ps_o[D * hh:D * hh + D, hh, :, 0:QS * n])
            mm.then_inc(done, 1)

        @block.vector
        def _(dve):
            dve.memset(zero_sb[:], 0.0).then_inc(s_zero, 1)
            dve.memset(half_sb[:], -0.5).then_inc(s_init, 1)
            kt = k_pad[:].tensor
            for g in range(G):
                for n in range(KIMG + 1):
                    at = g * KFLAT + n * (H + HALO) * PW
                    dve.memset(bass.AP(kt, at, [[G * KFLAT, P], [1, HALO * PW]]), 0.0).then_inc(s_rows, 1)
            for count in due(s_rows, G * (KIMG + 1)):
                dve.wait_ge(s_rows, count)
            dve.memset(bass.AP(kt, 0, [[G * KFLAT, P], [KFLAT, G], [PW, KROWS + 1], [1, HALO]]), 0.0).then_inc(s_init, 1)
            for count in due(s_w, 16 * 14):
                dve.wait_ge(s_w, count)

            def moments(src, st, mv, var, sems, b, eps):
                stats, agg, done = sems
                for h in range(2):
                    dve.bn_stats(st[0:HT, h, :], src[0:HT, h, :]).then_inc(stats, 1)
                for count in due(stats, b.lin(2, 2), dve):
                    dve.wait_ge(stats, count)
                for h in range(2):
                    dve.bn_aggr(mv[0:HT, h, :], st[0:HT, h, :]).then_inc(agg, 1)
                for count in due(agg, b.lin(2, 2)):
                    dve.wait_ge(agg, count)
                dve.tensor_scalar(var[0:HT, :], mv[0:HT, :, 1], eps, None, ALU.add).then_inc(done, 1)

            def body(j):
                for k in range(4):
                    b, kb = lag(j, k, 4)
                    if b.inside:
                        gather_heads(dve, dve.tensor_copy, b, kb, (0, 1), exd)
                    if j.inside:
                        for count in due(qk, j.lin(4, k + 1)):
                            dve.wait_ge(qk, count)
                        for count in due(tr, j.lin(4, k - 3)):
                            dve.wait_ge(tr, count)
                        n = TB[k]
                        dve.scalar_tensor_tensor(out=s_sb[:, k, 0:n, :], in0=ps_s[k % 2][:, 0:n, 0:KK], scalar=SCALE,
                                                 in1=mask_sb[:].broadcast_to([P, n, KK]), op0=ALU.mult,
                                                 op1=ALU.add).then_inc(msa, 1)
                        for count in due(msa, j.lin(4, k + 1)):
                            dve.wait_ge(msa, count)
                        dve.tensor_reduce(mx[:, k, 0:n], s_sb[:, k, 0:n, :], AX.X, ALU.max).then_inc(ms, 1)
                    b, kb = lag(j, k, 1)
                    if b.inside:
                        for count in due(exp, b.lin(4, kb + 1)):
                            dve.wait_ge(exp, count)
                        n = TB[kb]
                        dve.tensor_reduce(sm[:, kb, 0:n], s_sb[:, kb, 0:n, :], AX.X, ALU.add).then_inc(sms, 1)
                        for count in due(sms, b.lin(4, kb + 1)):
                            dve.wait_ge(sms, count)
                        for count in due(nrm, b.lin(4, kb - 3)):
                            dve.wait_ge(nrm, count)
                        dve.reciprocal(rs[:, kb, 0:n], sm[:, kb, 0:n]).then_inc(rcp, 1)
                    o, n2, n3 = j.at(-2), j.at(2), j.at(3)
                    if k == 0 and o.inside:
                        for count in due(yd, o.lin(1, 1)):
                            dve.wait_ge(yd, count)
                        for count in due(xb, o.lin(1, 1)):
                            dve.wait_ge(xb, count)
                        for count in due(x1st[o.parity], o.turn(16)):
                            dve.wait_ge(x1st[o.parity], count)
                        dve.tensor_tensor(x1_sb[0:HT, o.parity], ps_vy[0:HT], x_res[0:HT, o.parity],
                                          ALU.add).then_inc(x1, 1)
                        for count in due(x1, o.lin(1, 1)):
                            dve.wait_ge(x1, count)
                        moments(x1_sb[:, o.parity], st2, mv2, ve2, (bst2, agg2, var2), o, 1e-5)
                    if k == 1 and n2.inside:
                        for count in due(pvj, n2.lin(1, 1)):
                            dve.wait_ge(pvj, count)
                        for count in due(vst[n2.parity], n2.turn(64)):
                            dve.wait_ge(vst[n2.parity], count)
                        dve.tensor_tensor(v_sb[0:HT, n2.parity], ps_vy[0:HT],
                                          bv_sb[0:HT].broadcast_to([HT, 2, C]), ALU.add).then_inc(ve, 1)
                    if k == 1 and o.inside:
                        for count in due(rsq2, o.lin(1, 1)):
                            dve.wait_ge(rsq2, count)
                        for count in due(xnst[o.parity], o.turn(16)):
                            dve.wait_ge(xnst[o.parity], count)
                        for h in range(2):
                            dve.tensor_scalar(xn2[0:HT, o.parity, h, :], x1_sb[0:HT, o.parity, h, :],
                                              mv2[0:HT, h, 0:1], rs2[0:HT, h:h + 1], ALU.subtract,
                                              ALU.mult).then_inc(xn2_done, 1)
                    if k == 2 and n3.inside:
                        for count in due(xld[n3.parity], n3.turn(16, 16)):
                            dve.wait_ge(xld[n3.parity], count)
                        moments(x_in[:, n3.parity], st1, mv1, ve1, (bst1, agg1, var1), n3, 1e-6)
                    if k == 3 and n3.inside:
                        for count in due(rsq1, n3.lin(1, 1)):
                            dve.wait_ge(rsq1, count)
                        for count in due(tx, n3.lin(1)):
                            dve.wait_ge(tx, count)
                        for h in range(2):
                            dve.tensor_scalar(xn[0:HT, h, :], x_in[0:HT, n3.parity, h, :],
                                              mv1[0:HT, h, 0:1], rs1[0:HT, h:h + 1], ALU.subtract,
                                              ALU.mult).then_inc(xn_done, 1)
                    if k == 3 and o.inside:
                        for count in due(lg, o.lin(1, 1)):
                            dve.wait_ge(lg, count)
                        dst = bass.AP(logit[:].tensor, o.lin(2 * E), [[2 * NBANDS * E, HT], [E, 2], [1, E]])
                        dve.tensor_tensor(dst, ps_vy[0:HT, :, 0:E], gb_sb[0:HT].broadcast_to([HT, 2, E]),
                                          ALU.add).then_inc(lge, 1)

            run(dve, body)
            steps = [0]

            def step(ins):
                steps[0] += 1
                ins.then_inc(gate, 1)
                for count in due(gate, steps[0]):
                    dve.wait_ge(gate, count)

            for s_ in (pv, exa, lge, tx2e, qbd, nrm, ke):
                for count in due(s_, totals[id(s_)]):
                    dve.wait_ge(s_, count)
            for p in range(2):
                for count in due(x1st[p], totals[id(x1st[p])]):
                    dve.wait_ge(x1st[p], count)
                for count in due(xnst[p], totals[id(xnst[p])]):
                    dve.wait_ge(xnst[p], count)
            full = [HT, 2 * NBANDS, E]
            lgt, cws, gm, eq, oh, p2 = (t[0:HT] for t in (logit, cw, g_m, g_eq, g_oh, g_p2))
            wide = gm.unsqueeze(2).broadcast_to(full)
            prefs = pref_sb[0:HT].broadcast_to(full)
            step(dve.tensor_reduce(gm, lgt, AX.X, ALU.max))
            step(dve.tensor_tensor(lgt, lgt, wide, ALU.subtract))
            for count in due(gexp, 1):
                dve.wait_ge(gexp, count)
            step(dve.tensor_reduce(gm, lgt, AX.X, ALU.add))
            step(dve.reciprocal(gm, gm))
            step(dve.tensor_tensor(lgt, lgt, wide, ALU.mult))
            step(dve.tensor_reduce(gm, lgt, AX.X, ALU.max))
            step(dve.tensor_tensor(eq, lgt, wide, ALU.is_equal))
            step(dve.tensor_tensor(eq, eq, prefs, ALU.mult))
            step(dve.tensor_reduce(gm, eq, AX.X, ALU.max))
            step(dve.tensor_tensor(oh, eq, wide, ALU.is_equal))
            step(dve.scalar_tensor_tensor(out=p2, in0=oh, scalar=-4.0, in1=lgt, op0=ALU.mult, op1=ALU.add))
            step(dve.tensor_reduce(gm, p2, AX.X, ALU.max))
            step(dve.tensor_tensor(eq, p2, wide, ALU.is_equal))
            step(dve.tensor_tensor(eq, eq, prefs, ALU.mult))
            step(dve.tensor_reduce(gm, eq, AX.X, ALU.max))
            step(dve.tensor_tensor(p2, eq, wide, ALU.is_equal))
            step(dve.tensor_tensor(oh, oh, p2, ALU.add))
            step(dve.tensor_tensor(cws, lgt, oh, ALU.mult))

            def ffn(j):
                p = j.parity
                if not j.inside:
                    return
                for count in due(fct, j.lin(1, -1)):
                    dve.wait_ge(fct, count)
                for count in due(fa, j.lin(2 * E, -2 * E)):
                    dve.wait_ge(fa, count)
                src = bass.AP(cw[:].tensor, j.lin(2 * E), [[2 * NBANDS * E, HT], [1, 2 * E]])
                dve.tensor_copy(f_cw[0:HT, p].rearrange("p h e -> p (h e)"), src).then_inc(fcw, 1)
                for e in range(E):
                    if e == 3:
                        for count in due(fb, j.lin(1, 1)):
                            dve.wait_ge(fb, count)
                        for count in due(fa, j.lin(2 * E, 2 * e)):
                            dve.wait_ge(fa, count)
                        dve.tensor_tensor(f_acc[0:HT, p], f_acc[0:HT, p], pf_b[0:HT], ALU.add).then_inc(fbd, 1)
                        for count in due(fbd, j.lin(1, 1)):
                            dve.wait_ge(fbd, count)
                    if e == 0:
                        for count in due(fcw, j.lin(1, 1)):
                            dve.wait_ge(fcw, count)
                        for count in due(fal[p], j.turn(16, 16)):
                            dve.wait_ge(fal[p], count)
                    for count in due(fy, j.lin(E, e + 1)):
                        dve.wait_ge(fy, count)
                    for h in range(2):
                        for count in due(fa, j.lin(2 * E, 2 * e - 1 + h)):
                            dve.wait_ge(fa, count)
                        dve.scalar_tensor_tensor(out=f_acc[0:HT, p, h, :], in0=pf_y[e % 2][0:HT, h, :],
                                                 scalar=f_cw[0:HT, p, h, e:e + 1], in1=f_acc[0:HT, p, h, :],
                                                 op0=ALU.mult, op1=ALU.add).then_inc(fa, 1)

            run(dve, ffn)

        @block.scalar
        def _(act):
            for count in due(s_w, 16 * 14):
                act.wait_ge(s_w, count)
            for count in due(s_init, 3):
                act.wait_ge(s_init, count)

            def body(j):
                for k in range(4):
                    b, kb = lag(j, k, 3)
                    if b.inside:
                        for count in due(tr, b.lin(4, kb + 1)):
                            act.wait_ge(tr, count)
                        for count in due(pv, b.lin(4, kb - 1)):
                            act.wait_ge(pv, count)
                        n = TB[kb]
                        act.copy(pT[0:KK, kb % 2, 0:n, :], ps_t[kb % 2][0:KK, 0:n, :]).then_inc(evt, 1)
                    b, kb = lag(j, k, 4)
                    if b.inside:
                        gather_heads(act, act.copy, b, kb, (2, 3), exa)
                    b, kb = lag(j, k, 1)
                    if b.inside:
                        for count in due(sub, b.lin(4, kb + 1)):
                            act.wait_ge(sub, count)
                        n = TB[kb]
                        act.activation(s_sb[:, kb, 0:n, :], s_sb[:, kb, 0:n, :], ACT.Exp).then_inc(exp, 1)
                    n2, o = j.at(2), j.at(-2)
                    if k == 0 and n2.inside:
                        for count in due(tx, n2.lin(1, 1)):
                            act.wait_ge(tx, count)
                        for count in due(pk, n2.lin(1)):
                            act.wait_ge(pk, count)
                        for count in due(pvj, n2.lin(1)):
                            act.wait_ge(pvj, count)
                        act.copy(xnT[:], ps_tr[:].rearrange("p g h t -> p g (h t)")).then_inc(txe, 1)
                    if k == 1 and n2.inside:
                        for count in due(pq, n2.lin(1, 1)):
                            act.wait_ge(pq, count)
                        for count in due(qbd, j.lin(G, G)):
                            act.wait_ge(qbd, count)
                        for g in range(G):
                            mm = act.activation(q_sb[:, n2.parity, g], ps_qk[:, g], ACT.Identity, bias=bq_sb[:, g:g + 1])
                        mm.then_inc(qe, 1)
                    if k == 1 and o.inside:
                        for count in due(tx2, o.lin(1, 1)):
                            act.wait_ge(tx2, count)
                        for count in due(lg, o.lin(1)):
                            act.wait_ge(lg, count)
                        act.copy(xn2T[:], ps_tr[:].rearrange("p g h t -> p g (h t)")).then_inc(tx2e, 1)
                    if k == 2 and n2.inside:
                        for count in due(pk, n2.lin(1, 1)):
                            act.wait_ge(pk, count)
                        for g in range(G):
                            dst = bass.AP(k_pad[:].tensor, (n2.key_row() + HALO) * PW + (g * KFLAT + HALO),
                                          [[G * KFLAT, P], [PW, ROWS], [1, W]])
                            mm = act.activation(dst, ps_qk[:, g, :].rearrange("p (r c) -> p r c", r=ROWS),
                                                ACT.Identity, bias=bk_sb[:, g:g + 1])
                        mm.then_inc(ke, 1)

            run(act, body)
            for count in due(gate, 2):
                act.wait_ge(gate, count)
            act.activation(logit[0:HT], logit[0:HT], ACT.Exp).then_inc(gexp, 1)
            for count in due(s_w12, 16 * (2 * E + 2)):
                act.wait_ge(s_w12, count)

            def ffn(j):
                p = j.parity
                n = j.at(1)
                for e in range(E):
                    if j.inside:
                        for half in range(2):
                            for count in due(fh, j.lin(2 * E, 2 * e + half + 1)):
                                act.wait_ge(fh, count)
                            for count in due(fy, j.lin(E, e - 1)):
                                act.wait_ge(fy, count)
                            for i in range(2):
                                hc = 2 * half + i
                                mm = act.activation(f_hT[:, e % 2, hc, :], pf_h[half][:, i, :], ACT.Gelu,
                                                    bias=b1_sb[:, e, hc:hc + 1])
                            mm.then_inc(fg, 1)
                    if e == 0 and n.inside:
                        for count in due(ftx, n.lin(1, 1)):
                            act.wait_ge(ftx, count)
                        for count in due(fh, j.lin(2 * E)):
                            act.wait_ge(fh, count)
                        act.copy(f_xT[:, n.parity], pf_tr[:]).then_inc(ftxe, 1)
                    if e == 1 and j.inside:
                        for count in due(fct, j.lin(1, 1)):
                            act.wait_ge(fct, count)
                        for count in due(fb, j.lin(1)):
                            act.wait_ge(fb, count)
                        act.copy(f_cwT[:], pf_c[:]).then_inc(fcte, 1)

            run(act, ffn)

        @block.gpsimd
        def _(pool):
            pool.memset(q_bd[:], 0.0).then_inc(s_init, 1)
            for count in due(s_w, 16 * 14, pool):
                pool.wait_ge(s_w, count)
            for count in due(s_init, 3, pool):
                pool.wait_ge(s_init, count)

            def body(j):
                for k in range(4):
                    if j.inside:
                        for count in due(ms, j.lin(4, k + 1), pool):
                            pool.wait_ge(ms, count)
                        n = TB[k]
                        pool.tensor_tensor(s_sb[:, k, 0:n, :], s_sb[:, k, 0:n, :],
                                           mx[:, k, 0:n].unsqueeze(2).broadcast_to([P, n, KK]),
                                           ALU.subtract).then_inc(sub, 1)
                    b, kb = lag(j, k, 1)
                    if b.inside:
                        for count in due(rcp, b.lin(4, kb + 1), pool):
                            pool.wait_ge(rcp, count)
                        n = TB[kb]
                        pool.tensor_tensor(s_sb[:, kb, 0:n, :], s_sb[:, kb, 0:n, :],
                                           rs[:, kb, 0:n].unsqueeze(2).broadcast_to([P, n, KK]),
                                           ALU.mult).then_inc(nrm, 1)
                    o, n1, n3 = j.at(-2), j.at(1), j.at(3)
                    if k == 0 and o.inside:
                        for count in due(var2, o.lin(1, 1), pool):
                            pool.wait_ge(var2, count)
                        for count in due(xn2_done, o.lin(2), pool):
                            pool.wait_ge(xn2_done, count)
                        pool.tensor_tensor(rs2[0:HT, :], ve2[0:HT, :], half_sb[0:HT, :], ALU.pow).then_inc(rsq2, 1)
                    b = j.at(-1)
                    if k == 0 and b.inside:
                        for count in due(xrl[b.parity], b.turn(16, 16), pool):
                            pool.wait_ge(xrl[b.parity], count)
                        pool.tensor_tensor(x_res[0:HT, b.parity], x_res[0:HT, b.parity],
                                           bo_sb[0:HT].broadcast_to([HT, 2, C]), ALU.add).then_inc(xb, 1)
                    if k == 1 and n1.inside:
                        for count in due(qe, n1.lin(1, 1), pool):
                            pool.wait_ge(qe, count)
                        for count in due(qk, j.lin(4), pool):
                            pool.wait_ge(qk, count)
                        for g in range(G):
                            pool.tensor_tensor(
                                q_bd[:, n1.parity, g, :, HG * g:HG * g + HG, :],
                                q_sb[:, n1.parity, g].rearrange("p (t q) -> p t q", t=NT).unsqueeze(2).broadcast_to([P, NT, HG, QQ]),
                                own_sb[:].unsqueeze(1).unsqueeze(3).broadcast_to([P, NT, HG, QQ]),
                                ALU.mult).then_inc(qbd, 1)
                    if k == 2 and n3.inside:
                        for count in due(var1, n3.lin(1, 1), pool):
                            pool.wait_ge(var1, count)
                        for count in due(xn_done, n3.lin(2), pool):
                            pool.wait_ge(xn_done, count)
                        pool.tensor_tensor(rs1[0:HT, :], ve1[0:HT, :], half_sb[0:HT, :], ALU.pow).then_inc(rsq1, 1)

            run(pool, body)


def kernel(**inputs):
    import numpy as _np
    import concourse.bacc as _bacc
    from concourse import mybir as _mybir
    from concourse.bass_utils import run_bass_kernel_spmd as _run

    nc = _bacc.Bacc("TRN2", target_bir_lowering=False, num_devices=1)
    d = {k.replace("L0_", ""): _np.asarray(v) for k, v in inputs.items()}
    qr, qc = _np.divmod(_np.arange(QQ), QS)
    kr, kc = _np.divmod(_np.arange(KK), KS)
    dr, dc = kr[None] - qr[:, None], kc[None] - qc[:, None]
    near = (dr >= 0) & (dr < WIN) & (dc >= 0) & (dc < WIN)
    mask = _np.tile(_np.where(near, 0.0, NEG).astype(_np.float32), (HEADS, 1))
    own = _np.repeat(_np.eye(P * HEADS // d["x"].shape[-1], dtype=_np.float32), d["x"].shape[-1] // HEADS, axis=0)
    named = {
        "x": d["x"], "wqT": d["conv_wq"].T, "wkT": d["conv_wk"].T, "wvT": d["conv_wv"].T, "woT": d["conv_wo"].T,
        "bq": d["conv_bq"].reshape(-1, P).T, "bk": d["conv_bk"].reshape(-1, P).T, "bv": d["conv_bv"], "bo": d["conv_bo"],
        "gate_w": d["ffn_gate_w"], "gate_b": d["ffn_gate_b"], "mask": mask, "own": own, "ident": _np.eye(P, dtype=_np.float32),
        "pref": _np.arange(8, 0, -1, dtype=_np.float32), "W1": d["ffn_W1"], "b1": d["ffn_b1"].reshape(8, -1, P).transpose(2, 0, 1),
        "W2": d["ffn_W2"], "b2": d["ffn_b2"],
    }
    arrays, args = {}, []
    for name, a in named.items():
        a = _np.ascontiguousarray(a)
        arrays[f"in_{name}"] = a
        args.append(nc.dram_tensor(f"in_{name}", a.shape, _mybir.dt.from_np(a.dtype), kind="ExternalInput").ap())
    args.append(nc.dram_tensor("out_0", d["x"].shape, _mybir.dt.float32, kind="ExternalOutput").ap())
    build(nc, *args)
    r = _run(nc, [arrays], core_ids=[0])
    return r.results[0]["out_0"]
```

```python
from contextlib import ExitStack

import concourse.bass as bass
from concourse import mybir

ALU = mybir.AluOpType
ACT = mybir.ActivationFunctionType
AX = mybir.AxisListType
F32 = mybir.dt.float32
F32R = mybir.dt.float32r

WIN = 7
HALO = WIN // 2
HEADS = 8
ROWS = 4
QS = 4
KS = QS + WIN - 1
KK = KS * KS
QQ = QS * QS
P = 128
TB = [4, 4, 3, 3]
T0 = [0, 4, 8, 11]
ROW = 272
NEG = -1.0e30


class Band:

    def __init__(self, m, c, total, unroll=2):
        self.m, self.c, self.total, self.unroll = m, c, total, unroll
        self.static = isinstance(m, int)

    def at(self, d):
        return Band(self.m, self.c + d, self.total, self.unroll)

    @property
    def inside(self):
        return not self.static or 0 <= self.unroll * self.m + self.c < self.total

    def slot(self, ring):
        return self.c % ring

    @property
    def parity(self):
        return self.c % 2

    def lin(self, a, b=0):
        return self.m * (self.unroll * a) + (a * self.c + b)

    def turn(self, a, b=0, ring=2):
        return (self.m * (self.unroll // ring) + self.c // ring) * a + b

    def row(self, per_image):
        return self.lin(ROWS) + ((self.m + self.c // 2) // (per_image // 2)) * HALO

    def key_row(self, per_image):
        pair = self.m + self.c // 2
        return ((pair % per_image) * 2 + self.c % 2) * ROWS + (pair // (per_image // 2)) % 2 * HALO


def slots_of_expert(ntok):
    return -(-ntok // P) * P + P


def tiles_in_all(ntok, experts):
    return -(-(2 * ntok + experts * (P - 1)) // P // 4) * 4


def build(nc, x, wqT, wkT, wvT, woT, bq, bk, bv, bo, gate_w, gate_b, mask, own, ident, expert_no, first_slot, dummy, lower, numbers, tile_no, W1, b1, W2, b2, out):
    NIMG, H, W, C = x.shape
    NTOK = NIMG * H * W
    NB = H // ROWS
    NBANDS = NIMG * NB
    BT = ROWS * W
    HT = BT // 2
    NT = W // QS
    PW = W + HALO
    PROWS = NIMG * (H + HALO) + HALO
    FLAT = (PROWS + 1) * PW
    KIMG = min(NIMG, 2)
    KROWS = KIMG * (H + HALO) + HALO
    KFLAT = (KROWS + 1) * PW
    G = C // P
    HG = HEADS // G
    D = C // HEADS
    E = gate_w.shape[1]
    SCALE = float(D) ** -0.5
    assert sum(TB) == NT and NB % 2 == 0 and D == 32 and HT <= P

    with ExitStack() as ctx:
        def sb(name, shape, dt=F32):
            return ctx.enter_context(nc.sbuf_tensor(name, shape, dt))

        totals = {}

        def sem(name, total=None):
            s = ctx.enter_context(nc.semaphore(name))
            if total is not None:
                totals[id(s)] = total
            return s

        v_pad = nc.dram_tensor("v_pad", [FLAT, C], F32).ap()
        NS = slots_of_expert(NTOK)
        NU = tiles_in_all(NTOK, E)
        slots = nc.dram_tensor("slots", [E * NS + P, ROW], F32).ap()
        x_tok = x.rearrange("n h w c -> (n h w) c")
        x1_dram = out

        HID = W1.shape[2]
        HC = HID // P
        table = sb("table", [1, 2, NU], mybir.dt.int32)
        base_sb = sb("base_sb", [P, 1, E])
        num_sb = sb("num_sb", [P, 2])
        no_sb = sb("no_sb", [P, 1, E])
        tno_sb = sb("tno_sb", [1, NU])
        slot_base = sb("slot_base", [P, 2, E])
        id_sb = sb("id_sb", [P, P])
        zero_sb = sb("zero_sb", [P, 3 * C])
        WE = G * HID + HC * C
        b1_sb = sb("b1_sb", [P, E, HID])
        b2_sb = sb("b2_sb", [P, E, C])
        early = ExitStack()
        keep_sb = sb

        def sb(name, shape, dt=F32):
            return early.enter_context(nc.sbuf_tensor(name, shape, dt))

        def psum(name, shape):
            return early.enter_context(nc.psum_tensor(name, shape, F32))

        wq_sb = sb("wq_sb", [P, G, C])
        wk_sb = sb("wk_sb", [P, G, C])
        wv_sb = sb("wv_sb", [P, G, C])
        wo_sb = sb("wo_sb", [P, G, C])
        gw_sb = sb("gw_sb", [P, G, E])
        bq_sb = sb("bq_sb", [P, G])
        bk_sb = sb("bk_sb", [P, G])
        bv_sb = sb("bv_sb", [P, 1, C])
        bo_sb = sb("bo_sb", [P, 1, C])
        gb_sb = sb("gb_sb", [P, 1, E])
        mask_sb = sb("mask_sb", [P, 1, KK])
        own_sb = sb("own_sb", [P, HG])
        half_sb = sb("half_sb", [P, 2])

        k_pad = sb("k_pad", [P, G, KFLAT])
        x_in = sb("x_in", [P, 2, 2, C])
        st1 = sb("st1", [P, 2, 6])
        mv1 = sb("mv1", [P, 2, 2])
        ve1 = sb("ve1", [P, 2])
        rs1 = sb("rs1", [P, 2])
        xn = sb("xn", [P, 2, C])
        xnT = sb("xnT", [P, G, BT])
        q_sb = sb("q_sb", [P, 2, G, BT])
        q_bd = sb("q_bd", [P, 2, G, NT, HEADS, QQ])
        v_sb = sb("v_sb", [P, 2, 2, C])
        v_win = sb("v_win", [P, 2, NT, C])
        s_sb = sb("s_sb", [P, 4, 4, KK])
        mx = sb("mx", [P, 4, 4])
        sm = sb("sm", [P, 4, 4])
        rs = sb("rs", [P, 4, 4])
        pT = sb("pT", [P, 2, 4, P])
        oT = sb("oT", [P, 2, G * ROWS, W])
        x_res = sb("x_res", [P, 2, 2, C])
        x1_sb = sb("x1_sb", [P, 2, 2, C])
        st2 = sb("st2", [P, 2, 6])
        mv2 = sb("mv2", [P, 2, 2])
        ve2 = sb("ve2", [P, 2])
        rs2 = sb("rs2", [P, 2])
        xn2 = sb("xn2", [P, 2, 2, ROW])
        lg_sb = sb("lg_sb", [P, 2, 2, E])
        srt = sb("srt", [P, 2, E])
        top = sb("top", [P, 2, E], mybir.dt.uint32)
        dif = sb("dif", [P, 2, E])
        dsum = sb("dsum", [P, 2])
        dinv = sb("dinv", [P, 2])
        w2 = sb("w2", [P, 2, 2])
        topf = sb("topf", [P, 2, 2])
        ohk = sb("ohk", [P, 2, 2, E])
        ohz = sb("ohz", [P, 5, E])
        wk = sb("wk", [P, 2, 2, E])
        rank = sb("rank", [P, 2, E])
        pk8 = sb("pk8", [P, 2, 2, E])
        posf = sb("posf", [P, 4])
        pos = sb("pos", [P, 2, 4], mybir.dt.int32)
        low_sb = sb("low_sb", [P, P])
        ones_sb = sb("ones_sb", [P, P])
        xn2T = sb("xn2T", [P, G, BT])

        ps_tr_all = psum("ps_tr", [P, 512])
        ps_tr = ps_tr_all[:, 0:G * BT].rearrange("p (g h t) -> p g h t", g=G, h=2)
        ps_rk = ps_tr_all[:, G * BT:G * BT + 3 * E]
        ps_qk = psum("ps_qk", [P, G, BT])
        ps_vy = psum("ps_vy", [P, 2, C])
        ps_s = [psum(f"ps_s{i}", [P, 4, P]) for i in range(2)]
        ps_t = [psum(f"ps_t{i}", [P, 4, P]) for i in range(2)]
        ps_o = psum("ps_o", [P, HG, G * QS, 4 * QS])

        early.close()
        w_first = keep_sb("w_first", [P, 2, WE])
        w_hi = keep_sb("w_hi", [P, E, WE], F32R)
        w_lo = keep_sb("w_lo", [P, E, WE], F32R)
        sums = ExitStack()

        def sums_sb(name, shape, dt=F32):
            return sums.enter_context(nc.sbuf_tensor(name, shape, dt))

        t_ge = sums_sb("t_ge", [1, NU, E])
        t_cn = sums_sb("t_cn", [1, E])
        t_ci = sums_sb("t_ci", [1, E], mybir.dt.int32)
        t_ti = sums_sb("t_ti", [1, E], mybir.dt.int32)
        t_of = sums_sb("t_of", [1, NU])
        t_cu = sums_sb("t_cu", [1, 1, E])
        t_ex = sums_sb("t_ex", [1, NU])
        t_st = sums_sb("t_st", [1, NU])
        sums.close()
        f_x = keep_sb("f_x", [P, 4, ROW])
        f_id = keep_sb("f_id", [P, 4, 1], mybir.dt.int32)
        f_cw = keep_sb("f_cw", [P, 4, 1])
        f_xh = keep_sb("f_xh", [P, 2, G, P], F32R)
        f_xl = keep_sb("f_xl", [P, 2, G, P], F32R)
        f_b = keep_sb("f_b", [P, 4, C])
        with nc.sbuf_tensor("w_next", [P, 2, WE], F32) as w_next:
            pass
        f_h = keep_sb("f_h", [P, 2, HID])
        f_hh = keep_sb("f_hh", [P, 2, HC, P], F32R)
        f_hl = keep_sb("f_hl", [P, 2, HC, P], F32R)
        f_t = keep_sb("f_t", [P, 2, C])
        f_y = keep_sb("f_y", [P, 4, C])

        def staged(e):
            return (w_first if e % 4 < 2 else w_next)[:, e % 2]

        def late_psum(name, shape):
            return ctx.enter_context(nc.psum_tensor(name, shape, F32))

        pf_x = [late_psum(f"pf_x{i}", [P, G, P]) for i in range(2)]
        pf_h = [late_psum(f"pf_h{i}", [P, HID]) for i in range(2)]
        pf_t = [late_psum(f"pf_t{i}", [P, HC, P]) for i in range(2)]
        pf_y = [late_psum(f"pf_y{i}", [P, C]) for i in range(2)]

        NBAT = 4 * NBANDS
        s_w = sem("weights_loaded")
        s_zero = sem("zeros_made")
        s_rows = sem("key_pad_rows_cleared")
        s_init = sem("buffers_cleared")
        s_vz = sem("v_pads_stored")
        xld = [sem(f"x_loaded{p}", 16 * NBANDS // 2) for p in range(2)]
        xrl = [sem(f"residual_loaded{p}", 16 * NBANDS // 2) for p in range(2)]
        vst = [sem(f"v_stored{p}", 64 * NBANDS // 2) for p in range(2)]
        vwl = [sem(f"v_window_loaded{p}", 16 * KS * NBANDS // 2) for p in range(2)]
        x1st = [sem(f"x1_stored{p}", 16 * NBANDS // 2) for p in range(2)]
        sct = [sem(f"tokens_dispatched{p}", 64 * NBANDS // 2) for p in range(2)]
        qk = sem("scores_made", NBAT)
        msa = sem("scores_masked", NBAT)
        ms = sem("maxima_made", NBAT)
        exp = sem("exponentials_made", NBAT)
        rcp = sem("sums_inverted", NBAT)
        nrm = sem("probabilities_made", NBAT)
        tr = sem("probabilities_turned", NBAT)
        evt = sem("turned_probabilities_kept", NBAT)
        pv = sem("values_weighted", NBAT)
        exd = sem("heads_gathered_by_vector", NBAT)
        exa = sem("heads_gathered_by_scalar", NBAT)
        bst1 = sem("ln1_stats", 2 * NBANDS)
        agg1 = sem("ln1_moments", 2 * NBANDS)
        var1 = sem("ln1_variance", NBANDS)
        rsq1 = sem("ln1_scale", NBANDS)
        xn_done = sem("ln1_done", 2 * NBANDS)
        tx = sem("ln1_turned", NBANDS)
        txe = sem("ln1_turned_kept", NBANDS)
        pq = sem("q_made", NBANDS)
        qe = sem("q_kept", NBANDS)
        qbd = sem("q_spread", G * NBANDS)
        pvj = sem("v_made", NBANDS)
        ve = sem("v_kept", NBANDS)
        pk = sem("k_made", NBANDS)
        ke = sem("k_kept", NBANDS)
        yd = sem("attention_projected", NBANDS)
        xb = sem("residual_biased", NBANDS)
        x1 = sem("x1_made", NBANDS)
        bst2 = sem("ln2_stats", 2 * NBANDS)
        agg2 = sem("ln2_moments", 2 * NBANDS)
        var2 = sem("ln2_variance", NBANDS)
        rsq2 = sem("ln2_scale", NBANDS)
        xn2_done = sem("ln2_done", 2 * NBANDS)
        tx2 = sem("ln2_turned", NBANDS)
        tx2e = sem("ln2_turned_kept", NBANDS)
        lg = sem("logits_made", NBANDS)
        lge = sem("logits_kept", NBANDS)
        s_wl = [sem(f"expert_weights_loaded{p}") for p in range(4)]
        s_b = sem("expert_biases_loaded")
        s_wh = sem("expert_weights_high")
        s_wo = sem("expert_weights_low")
        s_num = sem("first_numbers_set")
        s_pads = sem("dummy_rows_stored")
        GATE = 20
        steps = sem("gate_steps", GATE * NBANDS)
        gex = sem("gate_exponentials", NBANDS)
        grk = sem("ranks_made", NBANDS)
        tab = sem("table_steps")
        fxl = [sem(f"slots_loaded{p}", 16 * NU // 4) for p in range(4)]
        fid = sem("slot_numbers_kept", 2 * NU)
        ftx = sem("slots_turned", NU)
        fxe = sem("slots_turned_high", NU)
        fxo = sem("slots_turned_low", NU)
        fh = sem("hidden_made", NU)
        fhb = sem("hidden_biased", NU)
        fge = sem("gelu_made", NU)
        fth = sem("hidden_turned", NU)
        fte = sem("hidden_turned_high", NU)
        fto = sem("hidden_turned_low", NU)
        fy = sem("expert_out_made", NU)
        fbk = sem("output_biases_kept", NU)
        fyt = sem("expert_out_weighted", NU)
        fyd = sem("expert_out_biased", NU)
        fst = sem("expert_out_added", 16 * NU)

        def due(s, value, alone=None):
            if isinstance(value, int):
                value = min(value, totals.get(id(s), value))
                return [value] if value > 0 else []
            if alone is not None:
                value = alone.lower_val(value)
                alone.wait_ge(s_zero, 1)
            return [value]

        def run(e, body, total=NBANDS, lead=4, after=3, unroll=2):
            first = -(-after // unroll)
            last = (total - lead) // unroll
            for c in range(-lead, unroll * first):
                body(Band(0, c, total, unroll))
            with e.Fori(first, last) as m:
                for c in range(unroll):
                    body(Band(m, c, total, unroll))
            for c in range(unroll * last, total + after):
                body(Band(0, c, total, unroll))

        TAB_STEPS = 15
        TILES = {"total": NU, "lead": 4, "after": 1, "unroll": 8}

        def experts(engine, first, last):
            loaded = {}

            def fetch(i, d):
                n = i.at(d)
                if not n.inside:
                    return
                if (n.static, n.c) not in loaded:
                    loaded[n.static, n.c] = nc.values_load(
                        table[0:1, 0, bass.ds(n.lin(1), 1)], engines=[engine], min_val=0, max_val=E - 1,
                        skip_runtime_bounds_check_because="the table is clamped to it")

            def begin(i):
                if not i.static and i.c == 0:
                    loaded.clear()
                for d in range(first, last + 1):
                    fetch(i, d)

            def of(n):
                return loaded[n.static, n.c]

            return begin, fetch, of

        def lag(j, k, d):
            n = k - d
            return j.at(n // 4), n % 4

        block = ctx.enter_context(nc.Block())

        @block.sync
        def _(sp):
            for dst, src in ((wq_sb, wqT), (wk_sb, wkT), (wv_sb, wvT), (wo_sb, woT), (gw_sb, gate_w)):
                sp.dma_start(dst[:], src.rearrange("(g p) n -> p g n", p=P)).then_inc(s_w, 16)
            for dst, src in ((bq_sb, bq), (bk_sb, bk)):
                sp.dma_start(dst[:], src).then_inc(s_w, 16)
            for dst, src, n in ((bv_sb, bv, C), (bo_sb, bo, C), (gb_sb, gate_b, E)):
                sp.dma_start(dst[:, 0], bass.AP(src.tensor, 0, [[0, P], [1, n]])).then_inc(s_w, 16)
            sp.dma_start(mask_sb[:, 0], mask).then_inc(s_w, 16)
            sp.dma_start(base_sb[:, 0], bass.AP(first_slot.tensor, 0, [[0, P], [1, E]])).then_inc(s_w, 16)
            sp.dma_start(slot_base[:, 1], bass.AP(first_slot.tensor, 0, [[0, P], [1, E]])).then_inc(s_w, 16)
            sp.dma_start(no_sb[:, 0], bass.AP(expert_no.tensor, 0, [[0, P], [1, E]])).then_inc(s_w, 16)
            sp.dma_start(tno_sb[:], bass.AP(tile_no.tensor, 0, [[NU, 1], [1, NU]])).then_inc(s_w, 16)
            sp.dma_start(num_sb[:], numbers).then_inc(s_w, 16)
            sp.dma_start(low_sb[:], lower).then_inc(s_w, 16)
            sp.dma_start(own_sb[:], own).then_inc(s_w, 16)
            sp.dma_start(id_sb[:], ident).then_inc(s_w, 16)
            n_vz = 16 * (2 + NIMG + 1)

            def load_expert(e):
                sp.dma_start(staged(e)[:, 0:G * HID].rearrange("p (g n) -> p g n", g=G),
                             W1[e].rearrange("(g p) n -> p g n", p=P)).then_inc(s_wl[e % 4], 16)
                sp.dma_start(staged(e)[:, G * HID:WE].rearrange("p (g n) -> p g n", g=HC),
                             W2[e].rearrange("(g p) n -> p g n", p=P)).then_inc(s_wl[e % 4], 16)

            def band_tokens(t, at):
                return bass.AP(t.tensor, at, [[C, HT], [HT * C, 2], [1, C]])

            def body(j):
                b = j.at(4)
                if b.inside:
                    for count in due(xn_done, j.at(4).lin(2, -2), sp):
                        sp.wait_ge(xn_done, count)
                    sp.dma_start(x_in[0:HT, b.parity], band_tokens(x_tok, j.at(4).lin(BT * C))).then_inc(xld[b.parity], 16)
                if j.static and j.c == -3:
                    for count in due(s_zero, 1, sp):
                        sp.wait_ge(s_zero, count)
                    vt = v_pad.tensor
                    n0 = PROWS // 2
                    sp.dma_start(bass.AP(vt, 0, [[PW * C, n0], [1, HALO * C]]), zero_sb[0:n0, :]).then_inc(s_vz, 16)
                    sp.dma_start(bass.AP(vt, n0 * PW * C, [[PW * C, PROWS + 1 - n0], [1, HALO * C]]),
                                 zero_sb[0:PROWS + 1 - n0, :]).then_inc(s_vz, 16)
                    for count in due(s_vz, 32, sp):
                        sp.wait_ge(s_vz, count)
                    for n in range(NIMG + 1):
                        sp.dma_start(bass.AP(vt, n * (H + HALO) * PW * C, [[HALO * C, PW], [1, HALO * C]]),
                                     zero_sb[0:PW, :]).then_inc(s_vz, 16)
                    sp.dma_start(out[NTOK:NTOK + P], zero_sb[:, 0:C]).then_inc(s_pads, 16)
                    sp.dma_start(slots[E * NS:E * NS + P], dummy).then_inc(s_pads, 16)
                if j.static and j.c == 0:
                    for dst, src, n in ((b1_sb, b1, HID), (b2_sb, b2, C)):
                        sp.dma_start(dst[:], bass.AP(src.tensor, 0, [[0, P], [1, E * n]])).then_inc(s_b, 16)
                if j.inside:
                    for count in due(x1, j.lin(1, -1), sp):
                        sp.wait_ge(x1, count)
                    sp.dma_start(x_res[0:HT, j.parity], band_tokens(x_tok, j.lin(BT * C))).then_inc(xrl[j.parity], 16)
                b = j.at(-2)
                if b.inside:
                    for count in due(x1, b.lin(1, 1), sp):
                        sp.wait_ge(x1, count)
                    sp.dma_start(band_tokens(x1_dram, b.lin(BT * C)), x1_sb[0:HT, b.parity]).then_inc(x1st[b.parity], 16)
                b = j.at(2)
                if b.inside:
                    for count in due(ve, b.lin(1, 1), sp):
                        sp.wait_ge(ve, count)
                    v_at = (b.row(NB) + HALO) * (PW * C)
                    for h in range(2):
                        for r in range(2):
                            sp.dma_start(
                                bass.AP(v_pad.tensor, v_at + ((2 * h + r) * PW + HALO) * C, [[C, W], [1, C]]),
                                v_sb[r * W:(r + 1) * W, b.parity, h, :]).then_inc(vst[b.parity], 16)
                b = j.at(1)
                if b.inside:
                    if j.static and j.c == -1:
                        for count in due(s_vz, n_vz, sp):
                            sp.wait_ge(s_vz, count)
                        for count in due(vst[0], 64, sp):
                            sp.wait_ge(vst[0], count)
                    for count in due(vst[j.parity], j.at(2).turn(64, 64), sp):
                        sp.wait_ge(vst[j.parity], count)
                    for count in due(pv, j.lin(4), sp):
                        sp.wait_ge(pv, count)
                    w_at = b.row(NB) * (PW * C)
                    for r in range(KS):
                        sp.dma_start(v_win[KS * r:KS * r + KS, b.parity],
                                     bass.AP(v_pad.tensor, w_at + r * PW * C, [[C, KS], [QS * C, NT], [1, C]])
                                     ).then_inc(vwl[b.parity], 16)

            run(sp, body)
            for p in range(2):
                for count in due(x1st[p], totals[id(x1st[p])], sp):
                    sp.wait_ge(x1st[p], count)
                for count in due(sct[p], totals[id(sct[p])], sp):
                    sp.wait_ge(sct[p], count)
            for last_use in (qk, pv, lge, exd, exa, tx2e, qbd, grk, steps, gex, lg):
                sp.wait_ge(last_use, totals[id(last_use)])
            for e in range(4):
                load_expert(e)
            sp.wait_ge(tab, 1)
            for e in range(E):
                if 4 <= e:
                    sp.wait_ge(s_wo, e - 3)
                    load_expert(e)
                end = nc.values_load(t_ci[0:1, e:e + 1], engines=[mybir.EngineType.SP], min_val=0, max_val=(E - 1) * NS + NTOK,
                                     skip_runtime_bounds_check_because="an expert has at most all tokens")
                sp.dma_start(bass.AP(slots.tensor, end * ROW, [[ROW, P], [1, ROW]]), dummy).then_inc(s_pads, 16)
            sp.wait_ge(s_pads, 16 * (2 + E))
            sp.wait_ge(tab, TAB_STEPS)

            def ffn(i):
                n = i.at(4)
                if n.inside:
                    for count in due(ftx, n.lin(1, -3), sp):
                        sp.wait_ge(ftx, count)
                    for count in due(fid, n.lin(2, -6), sp):
                        sp.wait_ge(fid, count)
                    first = nc.values_load(table[0:1, 1, bass.ds(n.lin(1), 1)], engines=[mybir.EngineType.SP], min_val=0,
                                           max_val=E * NS, skip_runtime_bounds_check_because="the table is clamped to it")
                    sp.dma_start(f_x[:, n.slot(4)], bass.AP(slots.tensor, first * ROW, [[ROW, P], [1, ROW]])
                                 ).then_inc(fxl[n.slot(4)], 16)

            run(sp, ffn, **TILES)
            sp.wait_ge(fst, 16 * NU)

        @block.tensor
        def _(pe):
            for count in due(s_w, 16 * 19):
                pe.wait_ge(s_w, count)
            for count in due(s_init, 3):
                pe.wait_ge(s_init, count)

            def turn(src, dst):
                for h in range(2):
                    for g in range(G):
                        mm = pe.transpose(dst[:, g, h, :], src[0:HT, h, P * g:P * g + P], id_sb[0:HT, 0:HT])
                return mm

            def body(j):
                for k in range(4):
                    if j.inside:
                        if k == 0:
                            for count in due(qbd, j.lin(G, G)):
                                pe.wait_ge(qbd, count)
                            for count in due(ke, j.lin(1, 2)):
                                pe.wait_ge(ke, count)
                        for count in due(msa, j.lin(4, k - 1)):
                            pe.wait_ge(msa, count)
                        row = j.key_row(NB) * PW
                        for t in range(TB[k]):
                            for g in range(G):
                                keys = bass.AP(k_pad[:].tensor, row + (g * KFLAT + QS * (T0[k] + t)),
                                               [[G * KFLAT, P], [PW, KS], [1, KS]])
                                qs = q_bd[:, j.parity, g, T0[k] + t].rearrange("p h q -> p (h q)")
                                mm = pe.matmul(ps_s[k % 2][:, t, 0:KK].rearrange("p (r c) -> p r c", r=KS),
                                               qs, keys, start=(g == 0), stop=(g == G - 1))
                        mm.then_inc(qk, 1)
                    b, kb = lag(j, k, 2)
                    if b.inside:
                        for count in due(nrm, b.lin(4, kb + 1)):
                            pe.wait_ge(nrm, count)
                        for count in due(evt, b.lin(4, kb - 1)):
                            pe.wait_ge(evt, count)
                        for t in range(TB[kb]):
                            mm = pe.transpose(ps_t[kb % 2][0:KK, t, :], s_sb[:, kb, t, :], id_sb[:, :])
                        mm.then_inc(tr, 1)
                    b, kb = lag(j, k, 3)
                    if b.inside:
                        for count in due(evt, b.lin(4, kb + 1)):
                            pe.wait_ge(evt, count)
                        for count in due(exd, b.lin(4, kb)):
                            pe.wait_ge(exd, count)
                        for count in due(exa, b.lin(4, kb)):
                            pe.wait_ge(exa, count)
                        if kb == 0:
                            for count in due(vwl[b.parity], b.turn(16 * KS, 16 * KS)):
                                pe.wait_ge(vwl[b.parity], count)
                        for t in range(TB[kb]):
                            for g in range(G):
                                dst = ps_o[:, :, QS * g:QS * g + QS, QS * t:QS * t + QS]
                                mm = pe.matmul(dst, v_win[0:KK, b.parity, T0[kb] + t, P * g:P * g + P],
                                               pT[0:KK, kb % 2, t, HG * QQ * g:HG * QQ * (g + 1)],
                                               start=True, stop=True)
                        mm.then_inc(pv, 1)
                    n, o = j.at(2), j.at(-2)
                    if k == 0 and n.inside:
                        for count in due(xn_done, n.lin(2, 2)):
                            pe.wait_ge(xn_done, count)
                        for count in due(tx2e, j.lin(1, -2)):
                            pe.wait_ge(tx2e, count)
                        turn(xn, ps_tr).then_inc(tx, 1)
                    if k == 1 and n.inside:
                        for count in due(txe, n.lin(1, 1)):
                            pe.wait_ge(txe, count)
                        for count in due(ke, n.lin(1)):
                            pe.wait_ge(ke, count)
                        for g in range(G):
                            for c in range(G):
                                dst = ps_qk[:, g, :].rearrange("p (t r c) -> p r t c", t=NT, r=QS)
                                mm = pe.matmul(dst, wq_sb[:, c, P * g:P * g + P], xnT[:, c, :],
                                               start=(c == 0), stop=(c == G - 1))
                        mm.then_inc(pq, 1)
                        for count in due(x1, j.lin(1, -1)):
                            pe.wait_ge(x1, count)
                        for h in range(2):
                            for c in range(G):
                                mm = pe.matmul(ps_vy[0:HT, h, :], xnT[:, c, HT * h:HT * h + HT], wv_sb[:, c, :],
                                               start=(c == 0), stop=(c == G - 1))
                        mm.then_inc(pvj, 1)
                    if k == 1 and o.inside:
                        for count in due(xn2_done, o.lin(2, 2)):
                            pe.wait_ge(xn2_done, count)
                        for count in due(txe, j.lin(1, 3)):
                            pe.wait_ge(txe, count)
                        turn(xn2[:, o.parity], ps_tr).then_inc(tx2, 1)
                    if k == 2 and n.inside:
                        for count in due(qe, n.lin(1, 1)):
                            pe.wait_ge(qe, count)
                        for g in range(G):
                            for c in range(G):
                                mm = pe.matmul(ps_qk[:, g, :], wk_sb[:, c, P * g:P * g + P], xnT[:, c, :],
                                               start=(c == 0), stop=(c == G - 1))
                        mm.then_inc(pk, 1)
                    if k == 2 and o.inside:
                        for count in due(tx2e, o.lin(1, 1)):
                            pe.wait_ge(tx2e, count)
                        for count in due(ve, j.lin(1, 3)):
                            pe.wait_ge(ve, count)
                        for h in range(2):
                            for c in range(G):
                                mm = pe.matmul(ps_vy[0:HT, h, 0:E], xn2T[:, c, HT * h:HT * h + HT], gw_sb[:, c, :],
                                               start=(c == 0), stop=(c == G - 1))
                        mm.then_inc(lg, 1)
                    o = j.at(-3)
                    if k == 2 and o.inside:
                        for count in due(steps, o.lin(GATE, 8)):
                            pe.wait_ge(steps, count)
                        for count in due(txe, j.lin(1, 3)):
                            pe.wait_ge(txe, count)
                        for count in due(tx2e, j.lin(1, -1)):
                            pe.wait_ge(tx2e, count)
                        for n_, (who, at) in enumerate(((low_sb, 2), (ones_sb, 1), (ones_sb, 0))):
                            mm = pe.matmul(ps_rk[0:HT, :], who[0:HT, 0:HT], ohz[0:HT, at:at + 3, :].rearrange("p a e -> p (a e)"),
                                           start=(n_ == 0), stop=(n_ == 2))
                        mm.then_inc(grk, 1)
                    b = j.at(-1)
                    if k == 3 and b.inside:
                        for count in due(exd, j.lin(4)):
                            pe.wait_ge(exd, count)
                        for count in due(exa, j.lin(4)):
                            pe.wait_ge(exa, count)
                        for count in due(lge, j.lin(1, -1)):
                            pe.wait_ge(lge, count)
                        for count in due(ve, j.lin(1, 3)):
                            pe.wait_ge(ve, count)
                        for h in range(2):
                            for g in range(G):
                                rows = slice(ROWS * g + 2 * h, ROWS * g + 2 * h + 2)
                                heads = oT[:, b.parity, rows, :].rearrange("p r c -> p (r c)")
                                mm = pe.matmul(ps_vy[0:HT, h, :], heads, wo_sb[:, g, :],
                                               start=(g == 0), stop=(g == G - 1))
                        mm.then_inc(yd, 1)

            run(pe, body)
            pe.wait_ge(s_wh, E)
            pe.wait_ge(s_wo, E)
            pe.wait_ge(tab, TAB_STEPS)

            begin, fetch, expert_of = experts(mybir.EngineType.PE, -1, 1)

            def ffn(i):
                begin(i)
                n = i.at(1)
                if n.inside:
                    e = expert_of(n)
                    for count in due(fxe, n.lin(1, 1)):
                        pe.wait_ge(fxe, count)
                    for count in due(fxo, n.lin(1, 1)):
                        pe.wait_ge(fxo, count)
                    for count in due(fhb, n.lin(1, -1)):
                        pe.wait_ge(fhb, count)
                    parts = [(x_, w_, c) for c in range(G) for x_, w_ in ((f_xh, w_hi), (f_xh, w_lo), (f_xl, w_hi))]
                    for at, (x_, w_, c) in enumerate(parts):
                        w = bass.AP(w_[:].tensor, e * WE + c * HID, [[E * WE, P], [1, HID]])
                        mm = pe.matmul(pf_h[n.parity][:], x_[:, n.parity, c, :], w, start=(at == 0), stop=(at == len(parts) - 1))
                    mm.then_inc(fh, 1)
                if i.c % 8 != 7:
                    fetch(i, 2)
                if i.inside:
                    for count in due(fge, i.lin(1, 1)):
                        pe.wait_ge(fge, count)
                    for count in due(fte, i.lin(1, -1)):
                        pe.wait_ge(fte, count)
                    for count in due(fto, i.lin(1, -1)):
                        pe.wait_ge(fto, count)
                    for hc in range(HC):
                        mm = pe.transpose(pf_t[i.parity][:, hc, :], f_h[:, i.parity, P * hc:P * hc + P], id_sb[:, :])
                    mm.then_inc(fth, 1)
                n = i.at(3)
                if n.inside:
                    for count in due(fxl[n.slot(4)], n.turn(16, 16, ring=4)):
                        pe.wait_ge(fxl[n.slot(4)], count)
                    for count in due(fxe, n.lin(1, -1)):
                        pe.wait_ge(fxe, count)
                    for count in due(fxo, n.lin(1, -1)):
                        pe.wait_ge(fxo, count)
                    for c in range(G):
                        mm = pe.transpose(pf_x[n.parity][:, c, :], f_x[:, n.slot(4), P * c:P * c + P], id_sb[:, :])
                    mm.then_inc(ftx, 1)
                b = i.at(-1)
                if b.inside:
                    e = expert_of(b)
                    for count in due(fte, b.lin(1, 1)):
                        pe.wait_ge(fte, count)
                    for count in due(fto, b.lin(1, 1)):
                        pe.wait_ge(fto, count)
                    for count in due(fyt, b.lin(1, -1)):
                        pe.wait_ge(fyt, count)
                    parts = [(h_, w_, hc) for hc in range(HC) for h_, w_ in ((f_hh, w_hi), (f_hh, w_lo), (f_hl, w_hi))]
                    for at, (h_, w_, hc) in enumerate(parts):
                        w = bass.AP(w_[:].tensor, e * WE + (G * HID + hc * C), [[E * WE, P], [1, C]])
                        mm = pe.matmul(pf_y[b.parity][:], h_[:, b.parity, hc, :], w, start=(at == 0), stop=(at == len(parts) - 1))
                    mm.then_inc(fy, 1)

            run(pe, ffn, **TILES)

        def gather_heads(e, copy, b, kb, hs, done):
            for count in due(pv, b.lin(4, kb + 1)):
                e.wait_ge(pv, count)
            if kb == 0:
                for count in due(yd, b.lin(1, -1)):
                    e.wait_ge(yd, count)
            n = TB[kb]
            for hh in hs:
                mm = copy(oT[D * hh:D * hh + D, b.parity, :, QS * T0[kb]:QS * (T0[kb] + n)],
                          ps_o[D * hh:D * hh + D, hh, :, 0:QS * n])
            mm.then_inc(done, 1)

        @block.vector
        def _(dve):
            dve.memset(zero_sb[:], 0.0).then_inc(s_zero, 1)
            dve.memset(ones_sb[:], 1.0).then_inc(s_rows, 1)
            dve.memset(xn2[:], 0.0).then_inc(s_rows, 1)
            dve.memset(ohz[:], 0.0).then_inc(s_rows, 1)
            dve.memset(half_sb[:], -0.5).then_inc(s_init, 1)
            kt = k_pad[:].tensor
            for g in range(G):
                for n in range(KIMG + 1):
                    at = g * KFLAT + n * (H + HALO) * PW
                    dve.memset(bass.AP(kt, at, [[G * KFLAT, P], [1, HALO * PW]]), 0.0).then_inc(s_rows, 1)
            for count in due(s_rows, G * (KIMG + 1) + 3):
                dve.wait_ge(s_rows, count)
            dve.memset(bass.AP(kt, 0, [[G * KFLAT, P], [KFLAT, G], [PW, KROWS + 1], [1, HALO]]), 0.0).then_inc(s_init, 1)
            for count in due(s_w, 16 * 19):
                dve.wait_ge(s_w, count)

            dve.tensor_copy(xn2[0:HT, 1, :, C + E], num_sb[0:HT, :]).then_inc(s_num, 1)
            dve.wait_ge(s_num, 1)

            def moments(src, st, mv, var, sems, b, eps):
                stats, agg, done = sems
                for h in range(2):
                    dve.bn_stats(st[0:HT, h, :], src[0:HT, h, :]).then_inc(stats, 1)
                for count in due(stats, b.lin(2, 2), dve):
                    dve.wait_ge(stats, count)
                for h in range(2):
                    dve.bn_aggr(mv[0:HT, h, :], st[0:HT, h, :]).then_inc(agg, 1)
                for count in due(agg, b.lin(2, 2)):
                    dve.wait_ge(agg, count)
                dve.tensor_scalar(var[0:HT, :], mv[0:HT, :, 1], eps, None, ALU.add).then_inc(done, 1)

            def body(j):
                for k in range(4):
                    b, kb = lag(j, k, 4)
                    if b.inside:
                        gather_heads(dve, dve.tensor_copy, b, kb, (0, 1), exd)
                    if j.inside:
                        for count in due(qk, j.lin(4, k + 1)):
                            dve.wait_ge(qk, count)
                        for count in due(tr, j.lin(4, k - 3)):
                            dve.wait_ge(tr, count)
                        n = TB[k]
                        dve.scalar_tensor_tensor(out=s_sb[:, k, 0:n, :], in0=ps_s[k % 2][:, 0:n, 0:KK], scalar=SCALE,
                                                 in1=mask_sb[:].broadcast_to([P, n, KK]), op0=ALU.mult,
                                                 op1=ALU.add).then_inc(msa, 1)
                        for count in due(msa, j.lin(4, k + 1)):
                            dve.wait_ge(msa, count)
                        dve.tensor_reduce(mx[:, k, 0:n], s_sb[:, k, 0:n, :], AX.X, ALU.max, negate=True).then_inc(ms, 1)
                    b, kb = lag(j, k, 1)
                    if b.inside:
                        for count in due(exp, b.lin(4, kb + 1)):
                            dve.wait_ge(exp, count)
                        n = TB[kb]
                        for count in due(nrm, b.lin(4, kb - 3)):
                            dve.wait_ge(nrm, count)
                        dve.reciprocal(rs[:, kb, 0:n], sm[:, kb, 0:n]).then_inc(rcp, 1)
                    o, n2, n3 = j.at(-2), j.at(2), j.at(3)
                    if k == 0 and o.inside:
                        for count in due(yd, o.lin(1, 1)):
                            dve.wait_ge(yd, count)
                        for count in due(xb, o.lin(1, 1)):
                            dve.wait_ge(xb, count)
                        for count in due(x1st[o.parity], o.turn(16)):
                            dve.wait_ge(x1st[o.parity], count)
                        dve.tensor_tensor(x1_sb[0:HT, o.parity], ps_vy[0:HT], x_res[0:HT, o.parity],
                                          ALU.add).then_inc(x1, 1)
                        for count in due(x1, o.lin(1, 1)):
                            dve.wait_ge(x1, count)
                        moments(x1_sb[:, o.parity], st2, mv2, ve2, (bst2, agg2, var2), o, 1e-5)
                    if k == 1 and o.inside:
                        for count in due(rsq2, o.lin(1, 1)):
                            dve.wait_ge(rsq2, count)
                        for count in due(sct[o.parity], o.turn(64)):
                            dve.wait_ge(sct[o.parity], count)
                        for h in range(2):
                            dve.tensor_scalar(xn2[0:HT, o.parity, h, 0:C], x1_sb[0:HT, o.parity, h, :],
                                              mv2[0:HT, h, 0:1], rs2[0:HT, h:h + 1], ALU.subtract,
                                              ALU.mult).then_inc(xn2_done, 1)
                    if k == 1 and n2.inside:
                        for count in due(pvj, n2.lin(1, 1)):
                            dve.wait_ge(pvj, count)
                        for count in due(vst[n2.parity], n2.turn(64)):
                            dve.wait_ge(vst[n2.parity], count)
                        dve.tensor_tensor(v_sb[0:HT, n2.parity], ps_vy[0:HT],
                                          bv_sb[0:HT].broadcast_to([HT, 2, C]), ALU.add).then_inc(ve, 1)
                    if k == 2 and n3.inside:
                        for count in due(xld[n3.parity], n3.turn(16, 16)):
                            dve.wait_ge(xld[n3.parity], count)
                        moments(x_in[:, n3.parity], st1, mv1, ve1, (bst1, agg1, var1), n3, 1e-6)
                    if k == 3 and n3.inside:
                        for count in due(rsq1, n3.lin(1, 1)):
                            dve.wait_ge(rsq1, count)
                        for count in due(tx, n3.lin(1)):
                            dve.wait_ge(tx, count)
                        for h in range(2):
                            dve.tensor_scalar(xn[0:HT, h, :], x_in[0:HT, n3.parity, h, :],
                                              mv1[0:HT, h, 0:1], rs1[0:HT, h:h + 1], ALU.subtract,
                                              ALU.mult).then_inc(xn_done, 1)
                    if k == 3 and o.inside:
                        for count in due(lg, o.lin(1, 1)):
                            dve.wait_ge(lg, count)
                        dst = lg_sb[0:HT, o.parity]
                        dve.tensor_tensor(dst, ps_vy[0:HT, :, 0:E], gb_sb[0:HT].broadcast_to([HT, 2, E]),
                                          ALU.add).then_inc(lge, 1)

                    o = j.at(-3)
                    if o.inside:
                        n_ = [{0: 0, 1: 5, 2: 8, 3: 14}[k]]

                        def step(ins):
                            n_[0] += 1
                            ins.then_inc(steps, 1)

                        def done():
                            return due(steps, o.lin(GATE, n_[0]), dve)

                        p, w = o.parity, slice(0, HT)
                        if k == 0:
                            for count in due(lge, o.lin(1, 1), dve):
                                dve.wait_ge(lge, count)
                            for h in range(2):
                                step(dve.max(srt[w, h, :], lg_sb[w, p, h, :]))
                            for count in done():
                                dve.wait_ge(steps, count)
                            for h in range(2):
                                step(dve.max_index(top[w, h, :], srt[w, h, :], lg_sb[w, p, h, :]))
                            step(dve.tensor_tensor(dif[w], srt[w], srt[w, :, 0:1].broadcast_to([HT, 2, E]), ALU.subtract))
                        if k == 1:
                            for count in done():
                                dve.wait_ge(steps, count)
                            step(dve.tensor_copy(topf[w], top[w, :, 0:2]))
                            for count in done():
                                dve.wait_ge(steps, count)
                            step(dve.tensor_tensor(ohk[w].rearrange("p h k e -> p (h k) e"), no_sb[w].broadcast_to([HT, 4, E]),
                                                   topf[w].rearrange("p h k -> p (h k)").unsqueeze(2).broadcast_to([HT, 4, E]),
                                                   ALU.is_equal))
                            for count in done():
                                dve.wait_ge(steps, count)
                            step(dve.tensor_tensor(ohz[w, 2:4], ohk[w, :, 0, :], ohk[w, :, 1, :], ALU.add))
                        if k == 2:
                            for count in due(gex, o.lin(1, 1)):
                                dve.wait_ge(gex, count)
                            step(dve.tensor_reduce(dsum[w], dif[w], AX.X, ALU.add))
                            for count in done():
                                dve.wait_ge(steps, count)
                            step(dve.reciprocal(dinv[w], dsum[w]))
                            for count in done():
                                dve.wait_ge(steps, count)
                            step(dve.tensor_tensor(w2[w], dif[w, :, 0:2], dinv[w].unsqueeze(2).broadcast_to([HT, 2, 2]), ALU.mult))
                            for count in done():
                                dve.wait_ge(steps, count)
                            step(dve.tensor_tensor(wk[w].rearrange("p h k e -> p (h k) e"), ohk[w].rearrange("p h k e -> p (h k) e"),
                                                   w2[w].rearrange("p h k -> p (h k)").unsqueeze(2).broadcast_to([HT, 4, E]),
                                                   ALU.mult))
                            for count in done():
                                dve.wait_ge(steps, count)
                            step(dve.tensor_tensor(xn2[w, p, :, C:C + E], wk[w, :, 0, :], wk[w, :, 1, :], ALU.add))
                            step(dve.tensor_scalar(xn2[w, p, :, C + E], xn2[w, 1 - p, :, C + E], float(BT), None, ALU.add))
                        if k == 3:
                            for count in due(grk, o.lin(1, 1)):
                                dve.wait_ge(grk, count)
                            step(dve.tensor_tensor(rank[w], ps_rk[w, 0:2 * E].rearrange("p (h e) -> p h e", h=2),
                                                   slot_base[w, 1 - p].unsqueeze(1).broadcast_to([HT, 2, E]), ALU.add))
                            step(dve.tensor_tensor(slot_base[w, p], slot_base[w, 1 - p], ps_rk[w, 2 * E:3 * E], ALU.add))
                            for count in done():
                                dve.wait_ge(steps, count)
                            for h in range(2):
                                step(dve.tensor_tensor(pk8[w, h], ohk[w, h], rank[w, h:h + 1, :].broadcast_to([HT, 2, E]), ALU.mult))
                            for count in done():
                                dve.wait_ge(steps, count)
                            step(dve.tensor_reduce(posf[w], pk8[w].rearrange("p h k e -> p (h k) e"), AX.X, ALU.add))
                            for count in done():
                                dve.wait_ge(steps, count)
                            step(dve.tensor_copy(pos[w, p], posf[w]))

            run(dve, body)
            last = (NBANDS - 1) % 2
            ends = slot_base[0:1, last, :]
            n_tab = [0]

            def link(ins):
                n_tab[0] += 1
                ins.then_inc(tab, 1)
                return n_tab[0]

            dve.wait_ge(steps, GATE * NBANDS)
            for used in (pv, exa, qe, txe, tx2e, qbd, nrm, ke, grk, gex, rsq2):
                dve.wait_ge(used, totals[id(used)])
            for p in range(2):
                dve.wait_ge(sct[p], totals[id(sct[p])])
                dve.wait_ge(x1st[p], totals[id(x1st[p])])
            dve.wait_ge(tab, link(dve.tensor_copy(t_ci[:], ends)))
            dve.wait_ge(tab, link(dve.scalar_tensor_tensor(out=t_cn[:], in0=ends, scalar=float(P - 1), in1=base_sb[0:1, 0, :],
                                                           op0=ALU.add, op1=ALU.subtract)))
            dve.wait_ge(tab, link(dve.tensor_copy(t_ti[:], t_cn[:])))
            dve.wait_ge(tab, link(dve.tensor_scalar(t_ti[:], t_ti[:], P.bit_length() - 1, None, ALU.logical_shift_right)))
            dve.wait_ge(tab, link(dve.tensor_copy(t_cn[:], t_ti[:])))
            dve.wait_ge(tab, link(dve.tensor_tensor_scan(t_cu[:, 0, :], t_cn[:], zero_sb[0:1, 0:E], 0.0, ALU.add, ALU.add)))
            wide = [1, NU, E]
            tno = tno_sb[:].unsqueeze(2).broadcast_to(wide)
            dve.wait_ge(tab, link(dve.tensor_tensor(t_ge[:], tno, t_cu[:].broadcast_to(wide), ALU.is_ge)))
            dve.wait_ge(tab, link(dve.tensor_reduce(t_ex[:], t_ge[:], AX.X, ALU.add)))
            dve.wait_ge(tab, link(dve.tensor_tensor(t_ge[:], t_ge[:], t_cu[:].broadcast_to(wide), ALU.mult)))
            dve.wait_ge(tab, link(dve.tensor_reduce(t_st[:], t_ge[:], AX.X, ALU.max)))
            dve.wait_ge(tab, link(dve.tensor_tensor(t_st[:], tno_sb[:], t_st[:], ALU.subtract)))
            dve.wait_ge(tab, link(dve.tensor_scalar(t_of[:], t_ex[:], float(NS), None, ALU.mult)))
            dve.wait_ge(tab, link(dve.scalar_tensor_tensor(out=t_of[:], in0=t_st[:], scalar=float(P), in1=t_of[:],
                                                           op0=ALU.mult, op1=ALU.add)))
            link(dve.tensor_scalar(table[:, 1, :], t_of[:], float(E * NS), None, ALU.min))
            link(dve.tensor_scalar(table[:, 0, :], t_ex[:], float(E - 1), None, ALU.min))
            assert n_tab[0] == TAB_STEPS
            dve.wait_ge(s_b, 32)
            for e in range(E):
                dve.wait_ge(s_wh, e + 1)
                dve.tensor_tensor(w_lo[:, e], staged(e), w_hi[:, e].bitcast(F32), ALU.subtract).then_inc(s_wo, 1)
            dve.wait_ge(tab, TAB_STEPS)

            begin, fetch, expert_of = experts(mybir.EngineType.DVE, 1, 1)

            def ffn(i):
                begin(i)
                n = i.at(1)
                if n.inside:
                    e = expert_of(n)
                    bias = bass.AP(b1_sb[:].tensor, e * HID, [[E * HID, P], [1, HID]])
                    for count in due(fh, n.lin(1, 1)):
                        dve.wait_ge(fh, count)
                    for count in due(fth, n.lin(1, -1)):
                        dve.wait_ge(fth, count)
                    dve.tensor_tensor(f_h[:, n.parity, :], pf_h[n.parity][:], bias, ALU.add).then_inc(fhb, 1)
                    bias = bass.AP(b2_sb[:].tensor, e * C, [[E * C, P], [1, C]])
                    for count in due(fyd, n.lin(1, -3), dve):
                        dve.wait_ge(fyd, count)
                    dve.tensor_copy(f_b[:, n.slot(4), :], bias).then_inc(fbk, 1)
                n = i.at(3)
                if n.inside:
                    for count in due(fxe, n.lin(1, 1)):
                        dve.wait_ge(fxe, count)
                    for count in due(fh, n.lin(1, -1)):
                        dve.wait_ge(fh, count)
                    dve.tensor_tensor(f_xl[:, n.parity], pf_x[n.parity][:], f_xh[:, n.parity].bitcast(F32), ALU.subtract).then_inc(fxo, 1)
                if i.inside:
                    for count in due(fte, i.lin(1, 1)):
                        dve.wait_ge(fte, count)
                    for count in due(fy, i.lin(1, -1)):
                        dve.wait_ge(fy, count)
                    dve.tensor_tensor(f_hl[:, i.parity], pf_t[i.parity][:], f_hh[:, i.parity].bitcast(F32), ALU.subtract).then_inc(fto, 1)

                b = i.at(-1)
                if b.inside:
                    for count in due(fyt, b.lin(1, 1)):
                        dve.wait_ge(fyt, count)
                    for count in due(fbk, b.lin(1, 1)):
                        dve.wait_ge(fbk, count)
                    for count in due(fst, b.lin(16, -32)):
                        dve.wait_ge(fst, count)
                    dve.scalar_tensor_tensor(out=f_y[:, b.slot(4), :], in0=f_b[:, b.slot(4), :], scalar=f_cw[:, b.slot(4), :],
                                             in1=f_t[:, b.parity, :], op0=ALU.mult, op1=ALU.add).then_inc(fyd, 1)

            run(dve, ffn, **TILES)

        @block.scalar
        def _(act):
            for count in due(s_w, 16 * 19):
                act.wait_ge(s_w, count)
            for count in due(s_init, 3):
                act.wait_ge(s_init, count)

            def body(j):
                for k in range(4):
                    b, kb = lag(j, k, 3)
                    if b.inside:
                        for count in due(tr, b.lin(4, kb + 1)):
                            act.wait_ge(tr, count)
                        for count in due(pv, b.lin(4, kb - 1)):
                            act.wait_ge(pv, count)
                        n = TB[kb]
                        act.copy(pT[0:KK, kb % 2, 0:n, :], ps_t[kb % 2][0:KK, 0:n, :]).then_inc(evt, 1)
                    b, kb = lag(j, k, 4)
                    if b.inside:
                        gather_heads(act, act.copy, b, kb, (2, 3), exa)
                    b, kb = lag(j, k, 1)
                    if b.inside:
                        for count in due(ms, b.lin(4, kb + 1)):
                            act.wait_ge(ms, count)
                        for t in range(TB[kb]):
                            mm = act.activation(s_sb[:, kb, t, :], s_sb[:, kb, t, :], ACT.Exp, bias=mx[:, kb, t:t + 1],
                                                accum_out=sm[:, kb, t:t + 1])
                        mm.then_inc(exp, 1)
                    n2, o = j.at(2), j.at(-2)
                    if k == 0 and n2.inside:
                        for count in due(tx, n2.lin(1, 1)):
                            act.wait_ge(tx, count)
                        for count in due(pk, n2.lin(1)):
                            act.wait_ge(pk, count)
                        for count in due(pvj, n2.lin(1)):
                            act.wait_ge(pvj, count)
                        act.copy(xnT[:], ps_tr.rearrange("p g h t -> p g (h t)")).then_inc(txe, 1)
                    if k == 1 and n2.inside:
                        for count in due(pq, n2.lin(1, 1)):
                            act.wait_ge(pq, count)
                        for count in due(qbd, j.lin(G, G)):
                            act.wait_ge(qbd, count)
                        for g in range(G):
                            mm = act.activation(q_sb[:, n2.parity, g], ps_qk[:, g], ACT.Identity, bias=bq_sb[:, g:g + 1])
                        mm.then_inc(qe, 1)
                    if k == 1 and o.inside:
                        for count in due(tx2, o.lin(1, 1)):
                            act.wait_ge(tx2, count)
                        for count in due(lg, o.lin(1)):
                            act.wait_ge(lg, count)
                        act.copy(xn2T[:], ps_tr.rearrange("p g h t -> p g (h t)")).then_inc(tx2e, 1)
                    if k == 2 and n2.inside:
                        for count in due(pk, n2.lin(1, 1)):
                            act.wait_ge(pk, count)
                        for g in range(G):
                            dst = bass.AP(k_pad[:].tensor, (n2.key_row(NB) + HALO) * PW + (g * KFLAT + HALO),
                                          [[G * KFLAT, P], [PW, ROWS], [1, W]])
                            mm = act.activation(dst, ps_qk[:, g, :].rearrange("p (r c) -> p r c", r=ROWS),
                                                ACT.Identity, bias=bk_sb[:, g:g + 1])
                        mm.then_inc(ke, 1)
                    o = j.at(-3)
                    if k == 1 and o.inside:
                        for count in due(steps, o.lin(GATE, 5)):
                            act.wait_ge(steps, count)
                        act.activation(dif[0:HT], dif[0:HT], ACT.Exp).then_inc(gex, 1)

            run(act, body)
            for used in (qk, pv, lge, exd, tx2e, qbd, grk, steps, lg):
                act.wait_ge(used, totals[id(used)])
            for p in range(2):
                act.wait_ge(sct[p], totals[id(sct[p])])
                act.wait_ge(x1st[p], totals[id(x1st[p])])
            for e in range(E):
                act.wait_ge(s_wl[e % 4], 32 * (e // 4 + 1))
                act.copy(w_hi[:, e], staged(e)).then_inc(s_wh, 1)
            act.wait_ge(tab, TAB_STEPS)

            def ffn(i):
                if i.inside:
                    for count in due(fth, i.lin(1, 1)):
                        act.wait_ge(fth, count)
                    for count in due(fy, i.lin(1, -1)):
                        act.wait_ge(fy, count)
                    act.copy(f_hh[:, i.parity], pf_t[i.parity][:]).then_inc(fte, 1)
                n = i.at(3)
                if n.inside:
                    for count in due(ftx, n.lin(1, 1)):
                        act.wait_ge(ftx, count)
                    for count in due(fh, n.lin(1, -1)):
                        act.wait_ge(fh, count)
                    act.copy(f_xh[:, n.parity], pf_x[n.parity][:]).then_inc(fxe, 1)
                n = i.at(1)
                if n.inside:
                    for count in due(fhb, n.lin(1, 1)):
                        act.wait_ge(fhb, count)
                    act.activation(f_h[:, n.parity, :], f_h[:, n.parity, :], ACT.Gelu).then_inc(fge, 1)
                b = i.at(-1)
                if b.inside:
                    for count in due(fy, b.lin(1, 1)):
                        act.wait_ge(fy, count)
                    for count in due(fid, b.lin(2, 2)):
                        act.wait_ge(fid, count)
                    for count in due(fyd, b.lin(1, -1)):
                        act.wait_ge(fyd, count)
                    act.activation(f_t[:, b.parity, :], pf_y[b.parity][:], ACT.Copy, scale=f_cw[:, b.slot(4), :]).then_inc(fyt, 1)

            run(act, ffn, **TILES)

        @block.gpsimd
        def _(pool):
            pool.memset(q_bd[:], 0.0).then_inc(s_init, 1)
            for count in due(s_w, 16 * 19, pool):
                pool.wait_ge(s_w, count)
            for count in due(s_init, 3, pool):
                pool.wait_ge(s_init, count)

            def body(j):
                for k in range(4):
                    b, kb = lag(j, k, 1)
                    if b.inside:
                        for count in due(rcp, b.lin(4, kb + 1), pool):
                            pool.wait_ge(rcp, count)
                        n = TB[kb]
                        pool.tensor_tensor(s_sb[:, kb, 0:n, :], s_sb[:, kb, 0:n, :],
                                           rs[:, kb, 0:n].unsqueeze(2).broadcast_to([P, n, KK]),
                                           ALU.mult).then_inc(nrm, 1)
                    o, n1, n3 = j.at(-2), j.at(1), j.at(3)
                    if k == 0 and o.inside:
                        for count in due(var2, o.lin(1, 1), pool):
                            pool.wait_ge(var2, count)
                        for count in due(xn2_done, o.lin(2), pool):
                            pool.wait_ge(xn2_done, count)
                        pool.tensor_tensor(rs2[0:HT, :], ve2[0:HT, :], half_sb[0:HT, :], ALU.pow).then_inc(rsq2, 1)
                    b = j.at(-1)
                    if k == 0 and b.inside:
                        for count in due(xrl[b.parity], b.turn(16, 16), pool):
                            pool.wait_ge(xrl[b.parity], count)
                        pool.tensor_tensor(x_res[0:HT, b.parity], x_res[0:HT, b.parity],
                                           bo_sb[0:HT].broadcast_to([HT, 2, C]), ALU.add).then_inc(xb, 1)
                    if k == 1 and n1.inside:
                        for count in due(qe, n1.lin(1, 1), pool):
                            pool.wait_ge(qe, count)
                        for count in due(qk, j.lin(4), pool):
                            pool.wait_ge(qk, count)
                        for g in range(G):
                            pool.tensor_tensor(
                                q_bd[:, n1.parity, g, :, HG * g:HG * g + HG, :],
                                q_sb[:, n1.parity, g].rearrange("p (t q) -> p t q", t=NT).unsqueeze(2).broadcast_to([P, NT, HG, QQ]),
                                own_sb[:].unsqueeze(1).unsqueeze(3).broadcast_to([P, NT, HG, QQ]),
                                ALU.mult).then_inc(qbd, 1)
                    if k == 2 and n3.inside:
                        for count in due(var1, n3.lin(1, 1), pool):
                            pool.wait_ge(var1, count)
                        for count in due(xn_done, n3.lin(2), pool):
                            pool.wait_ge(xn_done, count)
                        pool.tensor_tensor(rs1[0:HT, :], ve1[0:HT, :], half_sb[0:HT, :], ALU.pow).then_inc(rsq1, 1)
                    o = j.at(-3)
                    if k == 3 and o.inside:
                        for count in due(steps, o.lin(GATE, GATE), pool):
                            pool.wait_ge(steps, count)
                        for h in range(2):
                            for i in range(2):
                                pool.indirect_dma_start(
                                    slots, bass.IndirectOffsetOnAxis(ap=pos[0:HT, o.parity, 2 * h + i:2 * h + i + 1], axis=0),
                                    xn2[0:HT, o.parity, h, :], None).then_inc(sct[o.parity], 16)

            run(pool, body)
            for p in range(2):
                pool.wait_ge(x1st[p], totals[id(x1st[p])])
            pool.wait_ge(s_pads, 16 * (2 + E))
            pool.wait_ge(tab, TAB_STEPS)

            begin, fetch, expert_of = experts(mybir.EngineType.Pool, 1, 1)

            def ffn(i):
                begin(i)
                n = i.at(1)
                if n.inside:
                    for count in due(fxl[n.slot(4)], n.turn(16, 16, ring=4), pool):
                        pool.wait_ge(fxl[n.slot(4)], count)
                    for count in due(fst, n.lin(16, -48), pool):
                        pool.wait_ge(fst, count)
                    mine = bass.AP(f_x[:].tensor, expert_of(n) + (n.slot(4) * ROW + C), [[4 * ROW, P], [1, 1]])
                    pool.tensor_copy(f_cw[:, n.slot(4), :], mine).then_inc(fid, 1)
                    pool.tensor_copy(f_id[:, n.slot(4), :], f_x[:, n.slot(4), C + E:C + E + 1]).then_inc(fid, 1)
                b = i.at(-1)
                if b.inside:
                    for count in due(fyd, b.lin(1, 1), pool):
                        pool.wait_ge(fyd, count)
                    for count in due(fid, b.lin(2, 2), pool):
                        pool.wait_ge(fid, count)
                    for count in due(fst, b.lin(16), pool):
                        pool.wait_ge(fst, count)
                    pool.indirect_dma_start(out, bass.IndirectOffsetOnAxis(ap=f_id[:, b.slot(4), :], axis=0),
                                            f_y[:, b.slot(4), :], None, compute_op=ALU.add).then_inc(fst, 16)

            run(pool, ffn, **TILES)


def kernel(**inputs):
    import numpy as _np
    import concourse.bacc as _bacc
    from concourse import mybir as _mybir
    from concourse.bass_utils import run_bass_kernel_spmd as _run

    nc = _bacc.Bacc("TRN2", target_bir_lowering=False, num_devices=1)
    d = {k.replace("L0_", ""): _np.asarray(v) for k, v in inputs.items()}
    qr, qc = _np.divmod(_np.arange(QQ), QS)
    kr, kc = _np.divmod(_np.arange(KK), KS)
    dr, dc = kr[None] - qr[:, None], kc[None] - qc[:, None]
    near = (dr >= 0) & (dr < WIN) & (dc >= 0) & (dc < WIN)
    mask = _np.tile(_np.where(near, 0.0, NEG).astype(_np.float32), (HEADS, 1))
    own = _np.repeat(_np.eye(P * HEADS // d["x"].shape[-1], dtype=_np.float32), d["x"].shape[-1] // HEADS, axis=0)
    ntok, E = d["x"].size // d["x"].shape[-1], d["ffn_W1"].shape[0]
    dummy = _np.zeros((P, ROW), _np.float32)
    dummy[:, d["x"].shape[-1] + E] = ntok + _np.arange(P)
    ht = ROWS * d["x"].shape[2] // 2
    numbers = (_np.arange(P)[:, None] + ht * _np.arange(-2, 0)[None]).astype(_np.float32)
    named = {
        "x": d["x"], "wqT": d["conv_wq"].T, "wkT": d["conv_wk"].T, "wvT": d["conv_wv"].T, "woT": d["conv_wo"].T,
        "bq": d["conv_bq"].reshape(-1, P).T, "bk": d["conv_bk"].reshape(-1, P).T, "bv": d["conv_bv"], "bo": d["conv_bo"],
        "gate_w": d["ffn_gate_w"], "gate_b": d["ffn_gate_b"], "mask": mask, "own": own, "ident": _np.eye(P, dtype=_np.float32),
        "expert_no": _np.arange(E, dtype=_np.float32), "first_slot": _np.arange(E, dtype=_np.float32) * slots_of_expert(ntok),
        "dummy": dummy, "lower": _np.triu(_np.ones((P, P), _np.float32), 1), "numbers": numbers, "tile_no": _np.arange(tiles_in_all(ntok, E), dtype=_np.float32),
        "W1": d["ffn_W1"], "b1": d["ffn_b1"],
        "W2": d["ffn_W2"], "b2": d["ffn_b2"],
    }
    arrays, args = {}, []
    for name, a in named.items():
        a = _np.ascontiguousarray(a)
        arrays[f"in_{name}"] = a
        args.append(nc.dram_tensor(f"in_{name}", a.shape, _mybir.dt.from_np(a.dtype), kind="ExternalInput").ap())
    args.append(nc.dram_tensor("out_0", (ntok + P, d["x"].shape[-1]), _mybir.dt.float32, kind="ExternalOutput").ap())
    build(nc, *args)
    r = _run(nc, [arrays], core_ids=[0])
    return r.results[0]["out_0"][:ntok].reshape(d["x"].shape)
```

```python
from contextlib import ExitStack

import concourse.bass as bass
from concourse import mybir

ALU = mybir.AluOpType
ACT = mybir.ActivationFunctionType
AX = mybir.AxisListType
F32 = mybir.dt.float32
BF16 = mybir.dt.bfloat16
F32R = mybir.dt.float32r

WIN = 7
HALO = WIN // 2
HEADS = 8
ROWS = 4
QS = 4
KS = QS + WIN - 1
KK = KS * KS
QQ = QS * QS
P = 128
UW = 2 * QS + WIN - 1
UNITS = [3, 2, 2]
U0 = [0, 3, 5]
ROW = 272
NEG = -1.0e30


class Band:

    def __init__(self, m, c, total, unroll=2):
        self.m, self.c, self.total, self.unroll = m, c, total, unroll
        self.static = isinstance(m, int)

    def at(self, d):
        return Band(self.m, self.c + d, self.total, self.unroll)

    @property
    def inside(self):
        return not self.static or 0 <= self.unroll * self.m + self.c < self.total

    def slot(self, ring):
        return self.c % ring

    @property
    def parity(self):
        return self.c % 2

    def lin(self, a, b=0):
        return self.m * (self.unroll * a) + (a * self.c + b)

    def turn(self, a, b=0, ring=2):
        return (self.m * (self.unroll // ring) + self.c // ring) * a + b

    def row(self, per_image):
        return self.lin(ROWS) + ((self.m + self.c // 2) // (per_image // 2)) * HALO

    def key_row(self, per_image):
        return (((self.m + self.c // 2) % (per_image // 2)) * 2 + self.c % 2) * ROWS


def slots_of_expert(ntok):
    return -(-ntok // P) * P + P


def tiles_in_all(ntok, experts):
    return -(-(2 * ntok + experts * (P - 1)) // P // 4) * 4


def build(nc, x, wqT, wkT, wvT, woT, bq, bk, bv, bo, gate_w, gate_b, mask, own, ident, expert_no, first_slot, dummy, lower,
          numbers, tile_no, W1, b1, W2, b2, out):
    NIMG, H, W, C = x.shape
    NTOK = NIMG * H * W
    NB = H // ROWS
    NBANDS = NIMG * NB
    BT = ROWS * W
    HT = BT // 2
    NT = W // QS
    PW = W + HALO
    PROWS = NIMG * (H + HALO) + HALO
    FLAT = (PROWS + 1) * PW
    KROWS = H + 2 * HALO
    KFLAT = (KROWS + 1) * PW
    G = C // P
    BATS = G * len(UNITS)
    HG = HEADS // G
    D = C // HEADS
    E = gate_w.shape[1]
    SCALE = float(D) ** -0.5
    assert 2 * sum(UNITS) == NT and NB % 2 == 0 and D == 32 and HT <= P and G == 2 and E == 8

    with ExitStack() as ctx:
        def sb(name, shape, dt=F32):
            return ctx.enter_context(nc.sbuf_tensor(name, shape, dt))

        totals = {}

        def sem(name, total=None):
            s = ctx.enter_context(nc.semaphore(name))
            if total is not None:
                totals[id(s)] = total
            return s

        v_pad = nc.dram_tensor("v_pad", [FLAT, C], F32).ap()
        NS = slots_of_expert(NTOK)
        NU = tiles_in_all(NTOK, E)
        slots = nc.dram_tensor("slots", [E * NS + P, ROW], F32).ap()
        x_tok = x.rearrange("n h w c -> (n h w) c")

        HID = W1.shape[2]
        HC = HID // P
        table = sb("table", [1, 2, NU], mybir.dt.int32)
        base_sb = sb("base_sb", [P, 1, E])
        num_sb = sb("num_sb", [P, 2])
        no_sb = sb("no_sb", [P, 1, E])
        tno_sb = sb("tno_sb", [1, NU])
        slot_base = sb("slot_base", [P, 2, E])
        id_sb = sb("id_sb", [P, P])
        none_sb = sb("none_sb", [1, E])
        WE = G * HID + HC * C
        b1_sb = sb("b1_sb", [P, E, HID])
        b2_sb = sb("b2_sb", [P, E, C])
        w_first = sb("w_first", [P, 2, WE])
        xn2 = sb("xn2", [P, 2, 2, ROW])
        pos = sb("pos", [P, 2, 4], mybir.dt.int32)
        early = ExitStack()
        keep_sb = sb

        def sb(name, shape, dt=F32):
            return early.enter_context(nc.sbuf_tensor(name, shape, dt))

        def psum(name, shape):
            return early.enter_context(nc.psum_tensor(name, shape, F32))

        zero_sb = sb("zero_sb", [P, HALO * C])
        wq, wk_, wv, wo = ([sb(f"{name}_{part}", [P, G, C], F32R) for part in ("hi", "lo")] for name in ("wq", "wk", "wv", "wo"))
        gw_sb = sb("gw_sb", [P, G, E])
        bq_sb = sb("bq_sb", [P, G])
        bk_sb = sb("bk_sb", [P, G])
        bv_sb = sb("bv_sb", [P, 1, C])
        bo_sb = sb("bo_sb", [P, 1, C])
        gb_sb = sb("gb_sb", [P, 1, E])
        mask_sb = sb("mask_sb", [P, 1, KS, KS])
        own_sb = sb("own_sb", [P, HG])
        half_sb = sb("half_sb", [P, 2])

        k_pad = sb("k_pad", [P, G, KFLAT])
        x_in = sb("x_in", [P, 2, 2, C])
        st1 = sb("st1", [P, 2, 6])
        mv1 = sb("mv1", [P, 2, 2])
        ve1 = sb("ve1", [P, 2])
        rs1 = sb("rs1", [P, 2])
        xn = sb("xn", [P, 2, C])
        x_hl = [sb(f"xnT_{part}", [P, G, BT], F32R) for part in ("hi", "lo")]
        q_sb = sb("q_sb", [P, 2, G, BT])
        q_bd = sb("q_bd", [P, 2, G, NT, HG, QQ])
        v_sb = sb("v_sb", [P, 2, 2, C])
        with nc.sbuf_tensor("w_raw", [P, 4, G, C], F32) as w_raw:
            pass
        v_win = sb("v_win", [P, 2, NT, C])
        s_sb = sb("s_sb", [P, BATS, UNITS[0], KK])
        mx = sb("mx", [P, BATS, UNITS[0]])
        sm = sb("sm", [P, BATS, UNITS[0]])
        rs = sb("rs", [P, BATS, UNITS[0]])
        pT = sb("pT", [P, 2, UNITS[0], P])
        oT = sb("oT", [P, 2, G * ROWS, W])
        o_hl = [sb(f"oT_{part}", [P, G * ROWS, W], F32R) for part in ("hi", "lo")]
        x_res = sb("x_res", [P, 2, 2, C])
        x1_sb = sb("x1_sb", [P, 2, 2, C])
        st2 = sb("st2", [P, 2, 6])
        mv2 = sb("mv2", [P, 2, 2])
        ve2 = sb("ve2", [P, 2])
        rs2 = sb("rs2", [P, 2])
        lg_sb = sb("lg_sb", [P, 2, 2, E])
        srt = sb("srt", [P, 2, E])
        top = sb("top", [P, 2, E], mybir.dt.uint32)
        dif = sb("dif", [P, 2, E])
        dsum = sb("dsum", [P, 2])
        dinv = sb("dinv", [P, 2])
        w2 = sb("w2", [P, 2, 2])
        topf = sb("topf", [P, 2, 2])
        ohk = sb("ohk", [P, 2, 2, E])
        ohz = sb("ohz", [P, 5, E], BF16)
        wk = sb("wk", [P, 2, 2, E])
        rank = sb("rank", [P, 2, E])
        pk8 = sb("pk8", [P, 2, 2, E])
        posf = sb("posf", [P, 4])
        low_in = sb("low_in", [P, P])
        low_sb = sb("low_sb", [P, P], BF16)
        ones_sb = sb("ones_sb", [P, P], BF16)
        xn2T = sb("xn2T", [P, G, BT])

        ps_qk = psum("ps_qk", [P, G, BT])
        ps_tr = ps_qk[:].rearrange("p g (h t) -> p g h t", h=2)
        ps_vy = psum("ps_vy", [P, 2, C])
        ps_rk = ps_vy[:, 0, 0:3 * E]
        ps_s = [psum(f"ps_s{i}", [P, UNITS[0], KS, UW]) for i in range(2)]
        ps_t = [psum(f"ps_t{i}", [P, UNITS[0], P]) for i in range(2)]
        ps_o = [psum(f"ps_o{i}", [P, HG, QS, UNITS[0] * 2 * QS]) for i in range(2)]

        early.close()
        w_hi = keep_sb("w_hi", [P, E, WE], F32R)
        w_lo = keep_sb("w_lo", [P, E, WE], F32R)
        sums = ExitStack()

        def sums_sb(name, shape, dt=F32):
            return sums.enter_context(nc.sbuf_tensor(name, shape, dt))

        t_ge = sums_sb("t_ge", [1, NU, E])
        t_cn = sums_sb("t_cn", [1, E])
        t_ci = sums_sb("t_ci", [1, E], mybir.dt.int32)
        t_ti = sums_sb("t_ti", [1, E], mybir.dt.int32)
        t_of = sums_sb("t_of", [1, NU])
        t_cu = sums_sb("t_cu", [1, 1, E])
        t_ex = sums_sb("t_ex", [1, NU])
        t_st = sums_sb("t_st", [1, NU])
        sums.close()
        f_x = keep_sb("f_x", [P, 4, ROW])
        f_id = keep_sb("f_id", [P, 4, 1], mybir.dt.int32)
        f_cw = keep_sb("f_cw", [P, 4, 1])
        f_xh = keep_sb("f_xh", [P, 2, G, P], F32R)
        f_xl = keep_sb("f_xl", [P, 2, G, P], F32R)
        f_b = keep_sb("f_b", [P, 4, C])
        with nc.sbuf_tensor("w_next", [P, 2, WE], F32) as w_next:
            pass
        f_h = keep_sb("f_h", [P, 2, HID])
        f_hh = keep_sb("f_hh", [P, 2, HC, P], F32R)
        f_hl = keep_sb("f_hl", [P, 2, HC, P], F32R)
        f_t = keep_sb("f_t", [P, 2, C])
        f_y = keep_sb("f_y", [P, 4, C])

        ON_POOL = (2, 4)

        def staged(e):
            return (w_first if e % 4 < 2 else w_next)[:, e % 2]

        def low_made(e):
            return (expert_weights_low_by_gpsimd, e // 2) if e in ON_POOL else (expert_weights_low_by_vector, e + 1 - sum(o < e for o in ON_POOL))

        def late_psum(name, shape):
            return ctx.enter_context(nc.psum_tensor(name, shape, F32))

        pf_x = [late_psum(f"pf_x{i}", [P, G, P]) for i in range(2)]
        pf_h = [late_psum(f"pf_h{i}", [P, HID]) for i in range(2)]
        pf_t = [late_psum(f"pf_t{i}", [P, HC, P]) for i in range(2)]
        pf_y = [late_psum(f"pf_y{i}", [P, C]) for i in range(2)]

        NBAT = BATS * NBANDS
        weights_loaded = sem("weights_loaded")
        projection_weights_high = sem("projection_weights_high")
        projection_weights_low = sem("projection_weights_low")
        zeros_made = sem("zeros_made")
        key_pad_rows_cleared = sem("key_pad_rows_cleared")
        buffers_cleared = sem("buffers_cleared")
        v_pads_stored = sem("v_pads_stored")
        x_loaded = [sem(f"x_loaded{p}", 16 * NBANDS // 2) for p in range(2)]
        residual_loaded = [sem(f"residual_loaded{p}", 16 * NBANDS // 2) for p in range(2)]
        v_stored = [sem(f"v_stored{p}", 64 * NBANDS // 2) for p in range(2)]
        v_window_loaded = [sem(f"v_window_loaded{p}", 16 * KS * NBANDS // 2) for p in range(2)]
        x1_stored = [sem(f"x1_stored{p}", 16 * NBANDS // 2) for p in range(2)]
        tokens_dispatched = [sem(f"tokens_dispatched{p}", 64 * NBANDS // 2) for p in range(2)]
        scores_made = sem("scores_made", NBAT)
        scores_masked = sem("scores_masked", NBAT)
        maxima_made = sem("maxima_made", NBAT)
        exponentials_made = sem("exponentials_made", NBAT)
        sums_inverted = sem("sums_inverted", NBAT)
        probabilities_made = sem("probabilities_made", NBAT)
        probabilities_turned = sem("probabilities_turned", NBAT)
        turned_probabilities_kept = sem("turned_probabilities_kept", NBAT)
        values_weighted = sem("values_weighted", NBAT)
        heads_gathered_by_vector = sem("heads_gathered_by_vector", NBAT)
        heads_gathered_by_scalar = sem("heads_gathered_by_scalar", NBAT)
        ln1_stats = sem("ln1_stats", 2 * NBANDS)
        ln1_moments = sem("ln1_moments", 2 * NBANDS)
        ln1_variance = sem("ln1_variance", NBANDS)
        ln1_scale = sem("ln1_scale", NBANDS)
        ln1_done = sem("ln1_done", 2 * NBANDS)
        ln1_turned = sem("ln1_turned", NBANDS)
        ln1_turned_high = sem("ln1_turned_high", NBANDS)
        ln1_turned_low = sem("ln1_turned_low", NBANDS)
        heads_high = sem("heads_high", NBANDS)
        heads_low = sem("heads_low", NBANDS)
        q_made = sem("q_made", NBANDS)
        q_kept = sem("q_kept", NBANDS)
        q_spread = sem("q_spread", G * NBANDS)
        v_made = sem("v_made", NBANDS)
        v_kept = sem("v_kept", NBANDS)
        k_made = sem("k_made", NBANDS)
        k_kept = sem("k_kept", NBANDS)
        attention_projected = sem("attention_projected", NBANDS)
        residual_biased = sem("residual_biased", NBANDS)
        x1_made = sem("x1_made", NBANDS)
        ln2_stats = sem("ln2_stats", 2 * NBANDS)
        ln2_moments = sem("ln2_moments", 2 * NBANDS)
        ln2_variance = sem("ln2_variance", NBANDS)
        ln2_scale = sem("ln2_scale", NBANDS)
        ln2_done = sem("ln2_done", 2 * NBANDS)
        ln2_turned = sem("ln2_turned", NBANDS)
        ln2_turned_kept = sem("ln2_turned_kept", NBANDS)
        logits_made = sem("logits_made", NBANDS)
        logits_kept = sem("logits_kept", NBANDS)
        expert_weights_loaded = [sem(f"expert_weights_loaded{p}") for p in range(4)]
        expert_biases_loaded = sem("expert_biases_loaded")
        expert_weights_high = sem("expert_weights_high")
        expert_weights_low_by_vector = sem("expert_weights_low_by_vector")
        expert_weights_low_by_gpsimd = sem("expert_weights_low_by_gpsimd")
        first_numbers_set = sem("first_numbers_set")
        dummy_rows_stored = sem("dummy_rows_stored")
        GATE = 20
        gate_steps = sem("gate_steps", GATE * NBANDS)
        gate_exponentials = sem("gate_exponentials", NBANDS)
        ranks_made = sem("ranks_made", NBANDS)
        table_steps = sem("table_steps")
        slots_loaded = [sem(f"slots_loaded{p}", 16 * NU // 4) for p in range(4)]
        slot_numbers_kept = sem("slot_numbers_kept", 2 * NU)
        slots_turned = sem("slots_turned", NU)
        slots_turned_high = sem("slots_turned_high", NU)
        slots_turned_low = sem("slots_turned_low", NU)
        hidden_made = sem("hidden_made", NU)
        hidden_biased = sem("hidden_biased", NU)
        gelu_made = sem("gelu_made", NU)
        hidden_turned = sem("hidden_turned", NU)
        hidden_turned_high = sem("hidden_turned_high", NU)
        hidden_turned_low = sem("hidden_turned_low", NU)
        expert_out_made = sem("expert_out_made", NU)
        output_biases_kept = sem("output_biases_kept", NU)
        expert_out_weighted = sem("expert_out_weighted", NU)
        expert_out_biased = sem("expert_out_biased", NU)
        expert_out_added = sem("expert_out_added", 16 * NU)

        def due(s, value, alone=None):
            if isinstance(value, int):
                value = min(value, totals.get(id(s), value))
                return [value] if value > 0 else []
            if alone is not None:
                value = alone.lower_val(value)
                alone.wait_ge(zeros_made, 1)
            return [value]

        def run(e, body, total=NBANDS, lead=4, after=3, unroll=2):
            first = -(-after // unroll)
            last = (total - lead) // unroll
            for c in range(-lead, unroll * first):
                body(Band(0, c, total, unroll))
            with e.Fori(first, last) as m:
                for c in range(unroll):
                    body(Band(m, c, total, unroll))
            for c in range(unroll * last, total + after):
                body(Band(0, c, total, unroll))

        TAB_STEPS = 15
        TILES = {"total": NU, "lead": 4, "after": 1, "unroll": 12}

        def experts(engine, first, last):
            loaded = {}

            def fetch(i, d):
                n = i.at(d)
                if not n.inside:
                    return
                if (n.static, n.c) not in loaded:
                    loaded[n.static, n.c] = nc.values_load(
                        table[0:1, 0, bass.ds(n.lin(1), 1)], engines=[engine], min_val=0, max_val=E - 1,
                        skip_runtime_bounds_check_because="the table is clamped to it")

            def begin(i):
                if not i.static and i.c == 0:
                    loaded.clear()
                for d in range(first, last + 1):
                    fetch(i, d)

            def of(n):
                return loaded[n.static, n.c]

            return begin, fetch, of

        def lag(j, k, d):
            n = k - d
            return j.at(n // BATS), n % BATS

        block = ctx.enter_context(nc.Block())

        @block.sync
        def _(sp):
            for dst, src in ((w_raw[:, 0], wqT), (w_raw[:, 1], wkT), (w_raw[:, 2], wvT), (w_raw[:, 3], woT), (gw_sb[:], gate_w)):
                sp.dma_start(dst, src.rearrange("(g p) n -> p g n", p=P)).then_inc(weights_loaded, 16)
            for dst, src in ((bq_sb, bq), (bk_sb, bk)):
                sp.dma_start(dst[:], src).then_inc(weights_loaded, 16)
            for dst, src, n in ((bv_sb, bv, C), (bo_sb, bo, C), (gb_sb, gate_b, E)):
                sp.dma_start(dst[:, 0], bass.AP(src.tensor, 0, [[0, P], [1, n]])).then_inc(weights_loaded, 16)
            sp.dma_start(mask_sb[:, 0], mask).then_inc(weights_loaded, 16)
            sp.dma_start(base_sb[:, 0], bass.AP(first_slot.tensor, 0, [[0, P], [1, E]])).then_inc(weights_loaded, 16)
            sp.dma_start(slot_base[:, 1], bass.AP(first_slot.tensor, 0, [[0, P], [1, E]])).then_inc(weights_loaded, 16)
            sp.dma_start(no_sb[:, 0], bass.AP(expert_no.tensor, 0, [[0, P], [1, E]])).then_inc(weights_loaded, 16)
            sp.dma_start(tno_sb[:], bass.AP(tile_no.tensor, 0, [[NU, 1], [1, NU]])).then_inc(weights_loaded, 16)
            sp.dma_start(num_sb[:], numbers).then_inc(weights_loaded, 16)
            sp.dma_start(low_in[:], lower).then_inc(weights_loaded, 16)
            sp.dma_start(own_sb[:], own).then_inc(weights_loaded, 16)
            sp.dma_start(id_sb[:], ident).then_inc(weights_loaded, 16)
            n_vz = 16 * (2 + NIMG + 1)

            def load_expert(e):
                sp.dma_start(staged(e)[:, 0:G * HID].rearrange("p (g n) -> p g n", g=G),
                             W1[e].rearrange("(g p) n -> p g n", p=P)).then_inc(expert_weights_loaded[e % 4], 16)
                sp.dma_start(staged(e)[:, G * HID:WE].rearrange("p (g n) -> p g n", g=HC),
                             W2[e].rearrange("(g p) n -> p g n", p=P)).then_inc(expert_weights_loaded[e % 4], 16)

            def band_tokens(t, at):
                return bass.AP(t.tensor, at, [[C, HT], [HT * C, 2], [1, C]])

            def body(j):
                b = j.at(4)
                if b.inside:
                    for count in due(ln1_done, j.at(4).lin(2, -2), sp):
                        sp.wait_ge(ln1_done, count)
                    sp.dma_start(x_in[0:HT, b.parity], band_tokens(x_tok, j.at(4).lin(BT * C))).then_inc(x_loaded[b.parity], 16)
                if j.static and j.c == -3:
                    for count in due(zeros_made, 1, sp):
                        sp.wait_ge(zeros_made, count)
                    vt = v_pad.tensor
                    n0 = PROWS // 2
                    sp.dma_start(bass.AP(vt, 0, [[PW * C, n0], [1, HALO * C]]), zero_sb[0:n0, :]).then_inc(v_pads_stored, 16)
                    sp.dma_start(bass.AP(vt, n0 * PW * C, [[PW * C, PROWS + 1 - n0], [1, HALO * C]]),
                                 zero_sb[0:PROWS + 1 - n0, :]).then_inc(v_pads_stored, 16)
                    for count in due(v_pads_stored, 32, sp):
                        sp.wait_ge(v_pads_stored, count)
                    for n in range(NIMG + 1):
                        sp.dma_start(bass.AP(vt, n * (H + HALO) * PW * C, [[HALO * C, PW], [1, HALO * C]]),
                                     zero_sb[0:PW, :]).then_inc(v_pads_stored, 16)
                    sp.dma_start(out[NTOK:NTOK + P], zero_sb[:, 0:C]).then_inc(dummy_rows_stored, 16)
                    sp.dma_start(slots[E * NS:E * NS + P], dummy).then_inc(dummy_rows_stored, 16)
                if j.static and j.c == 1:
                    for dst, src, n in ((b1_sb, b1, HID), (b2_sb, b2, C)):
                        sp.dma_start(dst[:], bass.AP(src.tensor, 0, [[0, P], [1, E * n]])).then_inc(expert_biases_loaded, 16)
                if j.static and j.c in (2, 3):
                    load_expert(j.c - 2)
                if j.inside:
                    for count in due(x1_made, j.lin(1, -1), sp):
                        sp.wait_ge(x1_made, count)
                    sp.dma_start(x_res[0:HT, j.parity], band_tokens(x_tok, j.lin(BT * C))).then_inc(residual_loaded[j.parity], 16)
                b = j.at(-2)
                if b.inside:
                    for count in due(x1_made, b.lin(1, 1), sp):
                        sp.wait_ge(x1_made, count)
                    sp.dma_start(band_tokens(out, b.lin(BT * C)), x1_sb[0:HT, b.parity]).then_inc(x1_stored[b.parity], 16)
                b = j.at(2)
                if b.inside:
                    for count in due(v_kept, b.lin(1, 1), sp):
                        sp.wait_ge(v_kept, count)
                    v_at = (b.row(NB) + HALO) * (PW * C)
                    for h in range(2):
                        for r in range(2):
                            sp.dma_start(
                                bass.AP(v_pad.tensor, v_at + ((2 * h + r) * PW + HALO) * C, [[C, W], [1, C]]),
                                v_sb[r * W:(r + 1) * W, b.parity, h, :]).then_inc(v_stored[b.parity], 16)
                b = j.at(1)
                if b.inside:
                    if j.static and j.c == -1:
                        for count in due(v_pads_stored, n_vz, sp):
                            sp.wait_ge(v_pads_stored, count)
                        for count in due(v_stored[0], 64, sp):
                            sp.wait_ge(v_stored[0], count)
                    for count in due(v_stored[j.parity], j.at(2).turn(64, 64), sp):
                        sp.wait_ge(v_stored[j.parity], count)
                    for count in due(values_weighted, j.lin(BATS), sp):
                        sp.wait_ge(values_weighted, count)
                    w_at = b.row(NB) * (PW * C)
                    for r in range(KS):
                        sp.dma_start(v_win[KS * r:KS * r + KS, b.parity],
                                     bass.AP(v_pad.tensor, w_at + r * PW * C, [[C, KS], [QS * C, NT], [1, C]])
                                     ).then_inc(v_window_loaded[b.parity], 16)

            run(sp, body)
            for p in range(2):
                for count in due(x1_stored[p], totals[id(x1_stored[p])], sp):
                    sp.wait_ge(x1_stored[p], count)
            for last_use in (scores_made, values_weighted, logits_kept, heads_gathered_by_vector, heads_gathered_by_scalar, ln2_turned_kept, q_spread, ranks_made, gate_steps, gate_exponentials, logits_made):
                sp.wait_ge(last_use, totals[id(last_use)])
            for e in range(2, 4):
                load_expert(e)
            sp.wait_ge(*low_made(0))
            load_expert(4)
            sp.wait_ge(table_steps, 1)
            for p in range(2):
                sp.wait_ge(tokens_dispatched[p], totals[id(tokens_dispatched[p])])
            for e in range(E):
                end = nc.values_load(t_ci[0:1, e:e + 1], engines=[mybir.EngineType.SP], min_val=0, max_val=(E - 1) * NS + NTOK,
                                     skip_runtime_bounds_check_because="an expert has at most all tokens")
                sp.dma_start(bass.AP(slots.tensor, end * ROW, [[ROW, P], [1, ROW]]), dummy).then_inc(dummy_rows_stored, 16)
                if e == 2:
                    sp.wait_ge(*low_made(1))
                    load_expert(5)
            for e in range(6, E):
                sp.wait_ge(*low_made(e - 4))
                load_expert(e)
            sp.wait_ge(dummy_rows_stored, 16 * (2 + E))
            sp.wait_ge(table_steps, TAB_STEPS)

            def ffn(i):
                n = i.at(4)
                if n.inside:
                    for count in due(slots_turned, n.lin(1, -3), sp):
                        sp.wait_ge(slots_turned, count)
                    for count in due(slot_numbers_kept, n.lin(2, -6), sp):
                        sp.wait_ge(slot_numbers_kept, count)
                    first = nc.values_load(table[0:1, 1, bass.ds(n.lin(1), 1)], engines=[mybir.EngineType.SP], min_val=0,
                                           max_val=E * NS, skip_runtime_bounds_check_because="the table is clamped to it")
                    sp.dma_start(f_x[:, n.slot(4)], bass.AP(slots.tensor, first * ROW, [[ROW, P], [1, ROW]])
                                 ).then_inc(slots_loaded[n.slot(4)], 16)

            run(sp, ffn, **TILES)
            sp.wait_ge(expert_out_added, 16 * NU)

        @block.tensor
        def _(pe):
            for count in due(weights_loaded, 16 * 19):
                pe.wait_ge(weights_loaded, count)
            for count in due(buffers_cleared, 2):
                pe.wait_ge(buffers_cleared, count)

            pe.wait_ge(projection_weights_high, 4)
            pe.wait_ge(projection_weights_low, 5)

            def project(dst, weights, tokens, g):
                parts = [(w, x_, c) for w, x_ in ((0, 0), (1, 0), (0, 1)) for c in range(G)]
                for at, (w, x_, c) in enumerate(parts):
                    mm = pe.matmul(dst, weights[w][:, c, P * g:P * g + P], tokens[x_][:, c, :],
                                   start=(at == 0), stop=(at == len(parts) - 1))
                return mm

            def turn(src, dst):
                for h in range(2):
                    for g in range(G):
                        mm = pe.transpose(dst[:, g, h, :], src[0:HT, h, P * g:P * g + P], id_sb[0:HT, 0:HT])
                return mm

            def body(j):
                for k in range(BATS):
                    n, o, g3 = j.at(2), j.at(-2), j.at(-3)
                    if k == 0 and n.inside:
                        for count in due(ln1_done, n.lin(2, 2)):
                            pe.wait_ge(ln1_done, count)
                        for count in due(ln2_turned_kept, j.lin(1, -2)):
                            pe.wait_ge(ln2_turned_kept, count)
                        for count in due(k_kept, n.lin(1)):
                            pe.wait_ge(k_kept, count)
                        turn(xn, ps_tr).then_inc(ln1_turned, 1)
                    if j.inside:
                        if k == 0:
                            for count in due(q_spread, j.lin(G, G)):
                                pe.wait_ge(q_spread, count)
                            for count in due(k_kept, j.lin(1, 2)):
                                pe.wait_ge(k_kept, count)
                        for count in due(scores_masked, j.lin(BATS, k - 1)):
                            pe.wait_ge(scores_masked, count)
                        row = j.key_row(NB) * PW
                        g = k % G
                        for u in range(UNITS[k // G]):
                            pair = U0[k // G] + u
                            keys = bass.AP(k_pad[:].tensor, row + (g * KFLAT + 2 * QS * pair), [[G * KFLAT, P], [PW, KS], [1, UW]])
                            qs = q_bd[:, j.parity, g, 2 * pair:2 * pair + 2].rearrange("p t h q -> p (t h q)")
                            mm = pe.matmul(ps_s[k % 2][:, u], qs, keys, start=True, stop=True)
                        mm.then_inc(scores_made, 1)
                    b, kb = lag(j, k, 3)
                    if b.inside:
                        for count in due(probabilities_made, b.lin(BATS, kb + 1)):
                            pe.wait_ge(probabilities_made, count)
                        for count in due(turned_probabilities_kept, b.lin(BATS, kb - 1)):
                            pe.wait_ge(turned_probabilities_kept, count)
                        for u in range(UNITS[kb // G]):
                            mm = pe.transpose(ps_t[kb % 2][0:KK, u, :], s_sb[:, kb, u, :], id_sb[:, :])
                        mm.then_inc(probabilities_turned, 1)
                    b, kb = lag(j, k, 4)
                    if b.inside:
                        for count in due(turned_probabilities_kept, b.lin(BATS, kb + 1)):
                            pe.wait_ge(turned_probabilities_kept, count)
                        for count in due(heads_gathered_by_vector, b.lin(BATS, kb - 1)):
                            pe.wait_ge(heads_gathered_by_vector, count)
                        for count in due(heads_gathered_by_scalar, b.lin(BATS, kb - 1)):
                            pe.wait_ge(heads_gathered_by_scalar, count)
                        if kb == 0:
                            for count in due(v_window_loaded[b.parity], b.turn(16 * KS, 16 * KS)):
                                pe.wait_ge(v_window_loaded[b.parity], count)
                        g = kb % G
                        for u in range(UNITS[kb // G]):
                            for t in range(2):
                                dst = ps_o[kb % 2][:, :, :, QS * (2 * u + t):QS * (2 * u + t + 1)]
                                mm = pe.matmul(dst, v_win[0:KK, b.parity, 2 * (U0[kb // G] + u) + t, P * g:P * g + P],
                                               pT[0:KK, kb % 2, u, HG * QQ * t:HG * QQ * (t + 1)],
                                               start=True, stop=True)
                        mm.then_inc(values_weighted, 1)
                    if k == 1 and n.inside:
                        for count in due(ln1_turned_high, n.lin(1, 1)):
                            pe.wait_ge(ln1_turned_high, count)
                        for count in due(k_kept, n.lin(1)):
                            pe.wait_ge(k_kept, count)
                        for count in due(ln1_turned_low, n.lin(1, 1)):
                            pe.wait_ge(ln1_turned_low, count)
                        for g in range(G):
                            mm = project(ps_qk[:, g, :].rearrange("p (t r c) -> p r t c", t=NT, r=QS), wq, x_hl, g)
                        mm.then_inc(q_made, 1)
                    if k == 1 and g3.inside:
                        for count in due(gate_steps, g3.lin(GATE, 8)):
                            pe.wait_ge(gate_steps, count)
                        for count in due(x1_made, j.lin(1, -1)):
                            pe.wait_ge(x1_made, count)
                        for n_, (who, at) in enumerate(((low_sb, 2), (ones_sb, 1), (ones_sb, 0))):
                            mm = pe.matmul(ps_rk[0:HT, :], who[0:HT, 0:HT], ohz[0:HT, at:at + 3, :].rearrange("p a e -> p (a e)"),
                                           start=(n_ == 0), stop=(n_ == 2))
                        mm.then_inc(ranks_made, 1)
                    if k == 2 and n.inside:
                        for count in due(x1_made, j.lin(1, -1)):
                            pe.wait_ge(x1_made, count)
                        for count in due(gate_steps, g3.lin(GATE, 16)):
                            pe.wait_ge(gate_steps, count)
                        for h in range(2):
                            parts = [(x_, w, c) for c in range(G) for x_, w in ((0, 0), (0, 1), (1, 0))]
                            for at, (x_, w, c) in enumerate(parts):
                                mm = pe.matmul(ps_vy[0:HT, h, :], x_hl[x_][:, c, HT * h:HT * h + HT], wv[w][:, c, :],
                                               start=(at == 0), stop=(at == len(parts) - 1))
                        mm.then_inc(v_made, 1)
                    if k == 3 and o.inside:
                        for count in due(k_kept, j.lin(1, 3)):
                            pe.wait_ge(k_kept, count)
                        for count in due(ln2_done, o.lin(2, 2)):
                            pe.wait_ge(ln2_done, count)
                        for count in due(ln1_turned_high, j.lin(1, 3)):
                            pe.wait_ge(ln1_turned_high, count)
                        turn(xn2[:, o.parity], ps_tr).then_inc(ln2_turned, 1)
                    if k == 2 and n.inside:
                        for count in due(q_kept, n.lin(1, 1)):
                            pe.wait_ge(q_kept, count)
                        for g in range(G):
                            mm = project(ps_qk[:, g, :], wk_, x_hl, g)
                        mm.then_inc(k_made, 1)
                    if k == 4 and o.inside:
                        for count in due(ln2_turned_kept, o.lin(1, 1)):
                            pe.wait_ge(ln2_turned_kept, count)
                        for count in due(v_kept, j.lin(1, 3)):
                            pe.wait_ge(v_kept, count)
                        for h in range(2):
                            for c in range(G):
                                mm = pe.matmul(ps_vy[0:HT, h, 0:E], xn2T[:, c, HT * h:HT * h + HT], gw_sb[:, c, :],
                                               start=(c == 0), stop=(c == G - 1))
                        mm.then_inc(logits_made, 1)
                    b = j.at(-1)
                    if k == 5 and b.inside:
                        for count in due(heads_high, j.lin(1)):
                            pe.wait_ge(heads_high, count)
                        for count in due(heads_low, j.lin(1)):
                            pe.wait_ge(heads_low, count)
                        for count in due(logits_kept, j.lin(1, -1)):
                            pe.wait_ge(logits_kept, count)
                        for count in due(v_kept, j.lin(1, 3)):
                            pe.wait_ge(v_kept, count)
                        for h in range(2):
                            parts = [(x_, w, g) for g in range(G) for x_, w in ((0, 0), (0, 1), (1, 0))]
                            for at, (x_, w, g) in enumerate(parts):
                                rows = slice(ROWS * g + 2 * h, ROWS * g + 2 * h + 2)
                                heads = o_hl[x_][:, rows, :].rearrange("p r c -> p (r c)")
                                mm = pe.matmul(ps_vy[0:HT, h, :], heads, wo[w][:, g, :],
                                               start=(at == 0), stop=(at == len(parts) - 1))
                        mm.then_inc(attention_projected, 1)

            run(pe, body)
            pe.wait_ge(table_steps, TAB_STEPS)

            begin, fetch, expert_of = experts(mybir.EngineType.PE, -1, 1)

            def ffn(i):
                begin(i)
                n = i.at(1)
                if i.static and i.c == -1:
                    pe.wait_ge(expert_weights_high, E)
                    pe.wait_ge(expert_weights_low_by_vector, E - len(ON_POOL))
                    pe.wait_ge(expert_weights_low_by_gpsimd, len(ON_POOL))
                if n.inside:
                    e = expert_of(n)
                    for count in due(slots_turned_high, n.lin(1, 1)):
                        pe.wait_ge(slots_turned_high, count)
                    for count in due(slots_turned_low, n.lin(1, 1)):
                        pe.wait_ge(slots_turned_low, count)
                    for count in due(hidden_biased, n.lin(1, -1)):
                        pe.wait_ge(hidden_biased, count)
                    parts = [(x_, w_, c) for c in range(G) for x_, w_ in ((f_xh, w_hi), (f_xh, w_lo), (f_xl, w_hi))]
                    for at, (x_, w_, c) in enumerate(parts):
                        w = bass.AP(w_[:].tensor, e * WE + c * HID, [[E * WE, P], [1, HID]])
                        mm = pe.matmul(pf_h[n.parity][:], x_[:, n.parity, c, :], w, start=(at == 0), stop=(at == len(parts) - 1))
                    mm.then_inc(hidden_made, 1)
                if i.c % 12 != 11:
                    fetch(i, 2)
                if i.inside:
                    for count in due(gelu_made, i.lin(1, 1)):
                        pe.wait_ge(gelu_made, count)
                    for count in due(hidden_turned_high, i.lin(1, -1)):
                        pe.wait_ge(hidden_turned_high, count)
                    for count in due(hidden_turned_low, i.lin(1, -1)):
                        pe.wait_ge(hidden_turned_low, count)
                    for hc in range(HC):
                        mm = pe.transpose(pf_t[i.parity][:, hc, :], f_h[:, i.parity, P * hc:P * hc + P], id_sb[:, :])
                    mm.then_inc(hidden_turned, 1)
                n = i.at(3)
                if n.inside:
                    for count in due(slots_loaded[n.slot(4)], n.turn(16, 16, ring=4)):
                        pe.wait_ge(slots_loaded[n.slot(4)], count)
                    for count in due(slots_turned_high, n.lin(1, -1)):
                        pe.wait_ge(slots_turned_high, count)
                    for count in due(slots_turned_low, n.lin(1, -1)):
                        pe.wait_ge(slots_turned_low, count)
                    for c in range(G):
                        mm = pe.transpose(pf_x[n.parity][:, c, :], f_x[:, n.slot(4), P * c:P * c + P], id_sb[:, :])
                    mm.then_inc(slots_turned, 1)
                b = i.at(-1)
                if b.inside:
                    e = expert_of(b)
                    for count in due(hidden_turned_high, b.lin(1, 1)):
                        pe.wait_ge(hidden_turned_high, count)
                    for count in due(hidden_turned_low, b.lin(1, 1)):
                        pe.wait_ge(hidden_turned_low, count)
                    for count in due(expert_out_weighted, b.lin(1, -1)):
                        pe.wait_ge(expert_out_weighted, count)
                    parts = [(h_, w_, hc) for hc in range(HC) for h_, w_ in ((f_hh, w_hi), (f_hh, w_lo), (f_hl, w_hi))]
                    for at, (h_, w_, hc) in enumerate(parts):
                        w = bass.AP(w_[:].tensor, e * WE + (G * HID + hc * C), [[E * WE, P], [1, C]])
                        mm = pe.matmul(pf_y[b.parity][:], h_[:, b.parity, hc, :], w, start=(at == 0), stop=(at == len(parts) - 1))
                    mm.then_inc(expert_out_made, 1)

            run(pe, ffn, **TILES)

        def gather_heads(e, copy, b, kb, hs, done):
            for count in due(values_weighted, b.lin(BATS, kb + 1)):
                e.wait_ge(values_weighted, count)
            if kb == 0:
                for count in due(heads_high, b.lin(1, -1)):
                    e.wait_ge(heads_high, count)
                for count in due(heads_low, b.lin(1, -1)):
                    e.wait_ge(heads_low, count)
            g, first, n = kb % G, U0[kb // G], UNITS[kb // G]
            for hh in hs:
                mm = copy(oT[D * hh:D * hh + D, b.parity, ROWS * g:ROWS * (g + 1), 2 * QS * first:2 * QS * (first + n)],
                          ps_o[kb % 2][D * hh:D * hh + D, hh, :, 0:2 * QS * n])
            mm.then_inc(done, 1)

        @block.vector
        def _(dve):
            dve.memset(zero_sb[:], 0.0).then_inc(zeros_made, 1)
            dve.memset(none_sb[:], 0.0).then_inc(key_pad_rows_cleared, 1)
            dve.memset(ones_sb[:], 1.0).then_inc(key_pad_rows_cleared, 1)
            dve.memset(xn2[:], 0.0).then_inc(key_pad_rows_cleared, 1)
            dve.memset(ohz[:], 0.0).then_inc(key_pad_rows_cleared, 1)
            dve.memset(half_sb[:], -0.5).then_inc(buffers_cleared, 1)
            kt = k_pad[:].tensor
            for g in range(G):
                for n in range(2):
                    at = g * KFLAT + n * (H + HALO) * PW
                    dve.memset(bass.AP(kt, at, [[G * KFLAT, P], [1, HALO * PW]]), 0.0).then_inc(key_pad_rows_cleared, 1)
            for count in due(key_pad_rows_cleared, G * 2 + 4):
                dve.wait_ge(key_pad_rows_cleared, count)
            dve.memset(bass.AP(kt, 0, [[G * KFLAT, P], [KFLAT, G], [PW, KROWS + 1], [1, HALO]]), 0.0).then_inc(buffers_cleared, 1)
            for count in due(weights_loaded, 16 * 19):
                dve.wait_ge(weights_loaded, count)

            dve.tensor_copy(low_sb[:], low_in[:]).then_inc(projection_weights_low, 1)
            for at, w in enumerate((wq, wk_, wv, wo)):
                dve.wait_ge(projection_weights_high, at + 1)
                dve.tensor_tensor(w[1][:], w_raw[:, at], w[0][:].bitcast(F32), ALU.subtract).then_inc(projection_weights_low, 1)

            dve.tensor_copy(xn2[0:HT, 1, :, C + E], num_sb[0:HT, :]).then_inc(first_numbers_set, 1)
            dve.wait_ge(first_numbers_set, 1)

            def stats(src, st, done):
                for h in range(2):
                    dve.bn_stats(st[0:HT, h, :], src[0:HT, h, :]).then_inc(done, 1)

            def aggregate(st, made, mv, done, b):
                for count in due(made, b.lin(2, 2), dve):
                    dve.wait_ge(made, count)
                for h in range(2):
                    dve.bn_aggr(mv[0:HT, h, :], st[0:HT, h, :]).then_inc(done, 1)

            def variance(mv, made, var, eps, done, b):
                for count in due(made, b.lin(2, 2)):
                    dve.wait_ge(made, count)
                dve.tensor_scalar(var[0:HT, :], mv[0:HT, :, 1], eps, None, ALU.add).then_inc(done, 1)

            def normalise(dst, src, mv, rsd, h, done):
                dve.tensor_scalar(dst, src, mv[0:HT, h, 0:1], rsd[0:HT, h:h + 1], ALU.subtract, ALU.mult).then_inc(done, 1)

            def norms(j, at):
                o, n2, n3 = j.at(-2), j.at(2), j.at(3)
                if at == 1 and n2.inside:
                    for count in due(ln1_turned_high, n2.lin(1, 1)):
                        dve.wait_ge(ln1_turned_high, count)
                    for count in due(k_made, n2.lin(1)):
                        dve.wait_ge(k_made, count)
                    for count in due(v_made, n2.lin(1)):
                        dve.wait_ge(v_made, count)
                    dve.tensor_tensor(x_hl[1][:], ps_qk[:], x_hl[0][:].bitcast(F32), ALU.subtract).then_inc(ln1_turned_low, 1)
                if at == 1 and o.inside:
                    for count in due(attention_projected, o.lin(1, 1)):
                        dve.wait_ge(attention_projected, count)
                    for count in due(residual_biased, o.lin(1, 1)):
                        dve.wait_ge(residual_biased, count)
                    for count in due(x1_stored[o.parity], o.turn(16)):
                        dve.wait_ge(x1_stored[o.parity], count)
                    dve.tensor_tensor(x1_sb[0:HT, o.parity], ps_vy[0:HT], x_res[0:HT, o.parity],
                                      ALU.add).then_inc(x1_made, 1)
                if at == 3 and o.inside:
                    for count in due(x1_made, o.lin(1, 1)):
                        dve.wait_ge(x1_made, count)
                    stats(x1_sb[:, o.parity], st2, ln2_stats)
                if at == 4 and o.inside:
                    aggregate(st2, ln2_stats, mv2, ln2_moments, o)
                if at == 5 and o.inside:
                    variance(mv2, ln2_moments, ve2, 1e-5, ln2_variance, o)
                if at == 11 and n2.inside:
                    for count in due(v_made, n2.lin(1, 1)):
                        dve.wait_ge(v_made, count)
                    for count in due(v_stored[n2.parity], n2.turn(64)):
                        dve.wait_ge(v_stored[n2.parity], count)
                    dve.tensor_tensor(v_sb[0:HT, n2.parity], ps_vy[0:HT],
                                      bv_sb[0:HT].broadcast_to([HT, 2, C]), ALU.add).then_inc(v_kept, 1)
                if at in (9, 10) and o.inside:
                    h = at - 9
                    for count in due(ln2_scale, o.lin(1, 1)):
                        dve.wait_ge(ln2_scale, count)
                    for count in due(tokens_dispatched[o.parity], o.turn(64)):
                        dve.wait_ge(tokens_dispatched[o.parity], count)
                    normalise(xn2[0:HT, o.parity, h, 0:C], x1_sb[0:HT, o.parity, h, :], mv2, rs2, h, ln2_done)
                if at == 13 and n3.inside:
                    for count in due(x_loaded[n3.parity], n3.turn(16, 16)):
                        dve.wait_ge(x_loaded[n3.parity], count)
                    stats(x_in[:, n3.parity], st1, ln1_stats)
                if at == 14 and n3.inside:
                    aggregate(st1, ln1_stats, mv1, ln1_moments, n3)
                if at == 15 and n3.inside:
                    variance(mv1, ln1_moments, ve1, 1e-6, ln1_variance, n3)
                b = j.at(-1)
                if at == 20 and b.inside:
                    for count in due(heads_high, b.lin(1, 1)):
                        dve.wait_ge(heads_high, count)
                    for count in due(attention_projected, b.lin(1)):
                        dve.wait_ge(attention_projected, count)
                    dve.tensor_tensor(o_hl[1][:], oT[:, b.parity], o_hl[0][:].bitcast(F32), ALU.subtract).then_inc(heads_low, 1)
                if at == 19 and o.inside:
                    for count in due(logits_made, o.lin(1, 1)):
                        dve.wait_ge(logits_made, count)
                    dve.tensor_tensor(lg_sb[0:HT, o.parity], ps_vy[0:HT, :, 0:E], gb_sb[0:HT].broadcast_to([HT, 2, E]),
                                      ALU.add).then_inc(logits_kept, 1)
                if at in (21, 22) and n3.inside:
                    h = at - 21
                    for count in due(ln1_scale, n3.lin(1, 1)):
                        dve.wait_ge(ln1_scale, count)
                    for count in due(ln1_turned, n3.lin(1)):
                        dve.wait_ge(ln1_turned, count)
                    normalise(xn[0:HT, h, :], x_in[0:HT, n3.parity, h, :], mv1, rs1, h, ln1_done)

            BEFORE = {20: 0, 21: 2, 22: 5, 23: 6, 24: 7, 25: 8, 26: 9, 27: 10, 28: 11, 29: 12, 30: 14, 31: 16, 32: 18, 33: 19}

            def gate(j, at):
                o = j.at(-2)
                if at < 20:
                    o, at = j.at(-3), at + 24
                if not o.inside or at not in BEFORE:
                    return
                n_ = [BEFORE[at]]

                def step(ins):
                    n_[0] += 1
                    ins.then_inc(gate_steps, 1)

                p, w = o.parity, slice(0, HT)
                for count in due(gate_steps, o.lin(GATE, n_[0]), dve) if at > 20 else ():
                    dve.wait_ge(gate_steps, count)
                if at == 20:
                    for count in due(logits_kept, o.lin(1, 1), dve):
                        dve.wait_ge(logits_kept, count)
                    for h in range(2):
                        step(dve.max(srt[w, h, :], lg_sb[w, p, h, :]))
                if at == 21:
                    for h in range(2):
                        step(dve.max_index(top[w, h, :], srt[w, h, :], lg_sb[w, p, h, :]))
                    step(dve.tensor_tensor(dif[w], srt[w], srt[w, :, 0:1].broadcast_to([HT, 2, E]), ALU.subtract))
                if at == 22:
                    step(dve.tensor_copy(topf[w], top[w, :, 0:2]))
                if at == 23:
                    step(dve.tensor_tensor(ohk[w].rearrange("p h k e -> p (h k) e"), no_sb[w].broadcast_to([HT, 4, E]),
                                           topf[w].rearrange("p h k -> p (h k)").unsqueeze(2).broadcast_to([HT, 4, E]),
                                           ALU.is_equal))
                if at == 24:
                    step(dve.tensor_tensor(ohz[w, 2:4], ohk[w, :, 0, :], ohk[w, :, 1, :], ALU.add))
                if at == 25:
                    for count in due(gate_exponentials, o.lin(1, 1)):
                        dve.wait_ge(gate_exponentials, count)
                    step(dve.tensor_reduce(dsum[w], dif[w], AX.X, ALU.add))
                if at == 26:
                    step(dve.reciprocal(dinv[w], dsum[w]))
                if at == 27:
                    step(dve.tensor_tensor(w2[w], dif[w, :, 0:2], dinv[w].unsqueeze(2).broadcast_to([HT, 2, 2]), ALU.mult))
                if at == 28:
                    step(dve.tensor_tensor(wk[w].rearrange("p h k e -> p (h k) e"), ohk[w].rearrange("p h k e -> p (h k) e"),
                                           w2[w].rearrange("p h k -> p (h k)").unsqueeze(2).broadcast_to([HT, 4, E]),
                                           ALU.mult))
                if at == 29:
                    step(dve.tensor_tensor(xn2[w, p, :, C:C + E], wk[w, :, 0, :], wk[w, :, 1, :], ALU.add))
                    step(dve.tensor_scalar(xn2[w, p, :, C + E], xn2[w, 1 - p, :, C + E], float(BT), None, ALU.add))
                if at == 30:
                    for count in due(ranks_made, o.lin(1, 1)):
                        dve.wait_ge(ranks_made, count)
                    step(dve.tensor_tensor(rank[w], ps_rk[w, 0:2 * E].rearrange("p (h e) -> p h e", h=2),
                                           slot_base[w, 1 - p].unsqueeze(1).broadcast_to([HT, 2, E]), ALU.add))
                    step(dve.tensor_tensor(slot_base[w, p], slot_base[w, 1 - p], ps_rk[w, 2 * E:3 * E], ALU.add))
                if at == 31:
                    for h in range(2):
                        step(dve.tensor_tensor(pk8[w, h], ohk[w, h], rank[w, h:h + 1, :].broadcast_to([HT, 2, E]), ALU.mult))
                if at == 32:
                    step(dve.tensor_reduce(posf[w], pk8[w].rearrange("p h k e -> p (h k) e"), AX.X, ALU.add))
                if at == 33:
                    step(dve.tensor_copy(pos[w, p], posf[w]))

            def body(j):
                for k in range(BATS):
                    b, kb = lag(j, k, 5)
                    if b.inside:
                        gather_heads(dve, dve.tensor_copy, b, kb, (0, 1), heads_gathered_by_vector)
                    norms(j, 4 * k)
                    gate(j, 4 * k)
                    n, half = UNITS[k // G], HG * QQ
                    if j.inside:
                        for count in due(scores_made, j.lin(BATS, k + 1)):
                            dve.wait_ge(scores_made, count)
                        for count in due(probabilities_turned, j.lin(BATS, k + 1 - BATS)):
                            dve.wait_ge(probabilities_turned, count)
                        for t in range(2):
                            mm = dve.scalar_tensor_tensor(
                                out=s_sb[half * t:half * (t + 1), k, 0:n, :].rearrange("p n (r c) -> p n r c", r=KS),
                                in0=ps_s[k % 2][half * t:half * (t + 1), 0:n, :, QS * t:QS * t + KS], scalar=SCALE,
                                in1=mask_sb[half * t:half * (t + 1)].broadcast_to([half, n, KS, KS]), op0=ALU.mult, op1=ALU.add)
                        mm.then_inc(scores_masked, 1)
                    norms(j, 4 * k + 1)
                    gate(j, 4 * k + 1)
                    if j.inside:
                        for count in due(scores_masked, j.lin(BATS, k + 1)):
                            dve.wait_ge(scores_masked, count)
                        dve.tensor_reduce(mx[:, k, 0:n], s_sb[:, k, 0:n, :], AX.X, ALU.max, negate=True).then_inc(maxima_made, 1)
                    norms(j, 4 * k + 2)
                    gate(j, 4 * k + 2)
                    b, kb = lag(j, k, 1)
                    if b.inside:
                        for count in due(exponentials_made, b.lin(BATS, kb + 1)):
                            dve.wait_ge(exponentials_made, count)
                        n = UNITS[kb // G]
                        for count in due(probabilities_made, b.lin(BATS, kb + 1 - BATS)):
                            dve.wait_ge(probabilities_made, count)
                        dve.reciprocal(rs[:, kb, 0:n], sm[:, kb, 0:n]).then_inc(sums_inverted, 1)
                    norms(j, 4 * k + 3)
                    gate(j, 4 * k + 3)

            run(dve, body)
            last = (NBANDS - 1) % 2
            ends = slot_base[0:1, last, :]
            n_tab = [0]

            def link(ins):
                n_tab[0] += 1
                ins.then_inc(table_steps, 1)
                return n_tab[0]

            dve.wait_ge(gate_steps, GATE * NBANDS)
            for used in (values_weighted, heads_gathered_by_scalar, q_kept, ln1_turned_high, ln2_turned_kept, q_spread, probabilities_made, k_kept, ranks_made, gate_exponentials, ln2_scale):
                dve.wait_ge(used, totals[id(used)])
            for p in range(2):
                dve.wait_ge(x1_stored[p], totals[id(x1_stored[p])])
            dve.wait_ge(table_steps, link(dve.tensor_copy(t_ci[:], ends)))
            dve.wait_ge(table_steps, link(dve.scalar_tensor_tensor(out=t_cn[:], in0=ends, scalar=float(P - 1), in1=base_sb[0:1, 0, :],
                                                           op0=ALU.add, op1=ALU.subtract)))
            dve.wait_ge(table_steps, link(dve.tensor_copy(t_ti[:], t_cn[:])))
            dve.wait_ge(table_steps, link(dve.tensor_scalar(t_ti[:], t_ti[:], P.bit_length() - 1, None, ALU.logical_shift_right)))
            dve.wait_ge(table_steps, link(dve.tensor_copy(t_cn[:], t_ti[:])))
            dve.wait_ge(table_steps, link(dve.tensor_tensor_scan(t_cu[:, 0, :], t_cn[:], none_sb[:], 0.0, ALU.add, ALU.add)))
            wide = [1, NU, E]
            tno = tno_sb[:].unsqueeze(2).broadcast_to(wide)
            dve.wait_ge(table_steps, link(dve.tensor_tensor(t_ge[:], tno, t_cu[:].broadcast_to(wide), ALU.is_ge)))
            dve.wait_ge(table_steps, link(dve.tensor_reduce(t_ex[:], t_ge[:], AX.X, ALU.add)))
            dve.wait_ge(table_steps, link(dve.tensor_tensor(t_ge[:], t_ge[:], t_cu[:].broadcast_to(wide), ALU.mult)))
            dve.wait_ge(table_steps, link(dve.tensor_reduce(t_st[:], t_ge[:], AX.X, ALU.max)))
            dve.wait_ge(table_steps, link(dve.tensor_tensor(t_st[:], tno_sb[:], t_st[:], ALU.subtract)))
            dve.wait_ge(table_steps, link(dve.tensor_scalar(t_of[:], t_ex[:], float(NS), None, ALU.mult)))
            dve.wait_ge(table_steps, link(dve.scalar_tensor_tensor(out=t_of[:], in0=t_st[:], scalar=float(P), in1=t_of[:],
                                                           op0=ALU.mult, op1=ALU.add)))
            link(dve.tensor_scalar(table[:, 1, :], t_of[:], float(E * NS), None, ALU.min))
            link(dve.tensor_scalar(table[:, 0, :], t_ex[:], float(E - 1), None, ALU.min))
            assert n_tab[0] == TAB_STEPS
            dve.wait_ge(expert_biases_loaded, 32)
            for e in sorted(set(range(E)) - set(ON_POOL)):
                dve.wait_ge(expert_weights_high, e + 1)
                dve.tensor_tensor(w_lo[:, e], staged(e), w_hi[:, e].bitcast(F32), ALU.subtract).then_inc(expert_weights_low_by_vector, 1)
            dve.wait_ge(table_steps, TAB_STEPS)

            begin, fetch, expert_of = experts(mybir.EngineType.DVE, 1, 1)

            def ffn(i):
                begin(i)
                n = i.at(1)
                if n.inside:
                    e = expert_of(n)
                    bias = bass.AP(b1_sb[:].tensor, e * HID, [[E * HID, P], [1, HID]])
                    for count in due(hidden_made, n.lin(1, 1)):
                        dve.wait_ge(hidden_made, count)
                    for count in due(hidden_turned, n.lin(1, -1)):
                        dve.wait_ge(hidden_turned, count)
                    dve.tensor_tensor(f_h[:, n.parity, :], pf_h[n.parity][:], bias, ALU.add).then_inc(hidden_biased, 1)
                    bias = bass.AP(b2_sb[:].tensor, e * C, [[E * C, P], [1, C]])
                    for count in due(expert_out_biased, n.lin(1, -3), dve):
                        dve.wait_ge(expert_out_biased, count)
                    dve.tensor_copy(f_b[:, n.slot(4), :], bias).then_inc(output_biases_kept, 1)
                n = i.at(3)
                if n.inside:
                    for count in due(slots_turned_high, n.lin(1, 1)):
                        dve.wait_ge(slots_turned_high, count)
                    for count in due(hidden_made, n.lin(1, -1)):
                        dve.wait_ge(hidden_made, count)
                    dve.tensor_tensor(f_xl[:, n.parity], pf_x[n.parity][:], f_xh[:, n.parity].bitcast(F32), ALU.subtract).then_inc(slots_turned_low, 1)
                if i.inside:
                    for count in due(hidden_turned_high, i.lin(1, 1)):
                        dve.wait_ge(hidden_turned_high, count)
                    for count in due(expert_out_made, i.lin(1, -1)):
                        dve.wait_ge(expert_out_made, count)
                    dve.tensor_tensor(f_hl[:, i.parity], pf_t[i.parity][:], f_hh[:, i.parity].bitcast(F32), ALU.subtract).then_inc(hidden_turned_low, 1)

                b = i.at(-1)
                if b.inside:
                    for count in due(expert_out_weighted, b.lin(1, 1)):
                        dve.wait_ge(expert_out_weighted, count)
                    for count in due(output_biases_kept, b.lin(1, 1)):
                        dve.wait_ge(output_biases_kept, count)
                    for count in due(expert_out_added, b.lin(16, -32)):
                        dve.wait_ge(expert_out_added, count)
                    dve.scalar_tensor_tensor(out=f_y[:, b.slot(4), :], in0=f_b[:, b.slot(4), :], scalar=f_cw[:, b.slot(4), :],
                                             in1=f_t[:, b.parity, :], op0=ALU.mult, op1=ALU.add).then_inc(expert_out_biased, 1)

            run(dve, ffn, **TILES)

        @block.scalar
        def _(act):
            for count in due(weights_loaded, 16 * 19):
                act.wait_ge(weights_loaded, count)
            for count in due(buffers_cleared, 2):
                act.wait_ge(buffers_cleared, count)
            for at, w in enumerate((wq, wk_, wv, wo)):
                act.copy(w[0][:], w_raw[:, at]).then_inc(projection_weights_high, 1)

            def body(j):
                for k in range(BATS):
                    b, kb = lag(j, k, 4)
                    if b.inside:
                        for count in due(probabilities_turned, b.lin(BATS, kb + 1)):
                            act.wait_ge(probabilities_turned, count)
                        for count in due(values_weighted, b.lin(BATS, kb - 1)):
                            act.wait_ge(values_weighted, count)
                        n = UNITS[kb // G]
                        act.copy(pT[0:KK, kb % 2, 0:n, :], ps_t[kb % 2][0:KK, 0:n, :]).then_inc(turned_probabilities_kept, 1)
                    n2, o = j.at(2), j.at(-2)
                    if k == 0 and n2.inside:
                        for count in due(ln1_turned, n2.lin(1, 1)):
                            act.wait_ge(ln1_turned, count)
                        for count in due(k_made, n2.lin(1)):
                            act.wait_ge(k_made, count)
                        for count in due(v_made, n2.lin(1)):
                            act.wait_ge(v_made, count)
                        act.copy(x_hl[0][:], ps_qk[:]).then_inc(ln1_turned_high, 1)
                    if k == 2 and n2.inside:
                        for count in due(q_made, n2.lin(1, 1)):
                            act.wait_ge(q_made, count)
                        for count in due(q_spread, j.lin(G, G)):
                            act.wait_ge(q_spread, count)
                        for g in range(G):
                            mm = act.activation(q_sb[:, n2.parity, g], ps_qk[:, g], ACT.Identity, bias=bq_sb[:, g:g + 1])
                        mm.then_inc(q_kept, 1)
                    if k == 4 and o.inside:
                        for count in due(ln2_turned, o.lin(1, 1)):
                            act.wait_ge(ln2_turned, count)
                        for count in due(logits_made, o.lin(1)):
                            act.wait_ge(logits_made, count)
                        act.copy(xn2T[:], ps_tr.rearrange("p g h t -> p g (h t)")).then_inc(ln2_turned_kept, 1)
                    if k == 3 and n2.inside:
                        for count in due(k_made, n2.lin(1, 1)):
                            act.wait_ge(k_made, count)
                        for g in range(G):
                            dst = bass.AP(k_pad[:].tensor, (n2.key_row(NB) + HALO) * PW + (g * KFLAT + HALO),
                                          [[G * KFLAT, P], [PW, ROWS], [1, W]])
                            mm = act.activation(dst, ps_qk[:, g, :].rearrange("p (r c) -> p r c", r=ROWS),
                                                ACT.Identity, bias=bk_sb[:, g:g + 1])
                        mm.then_inc(k_kept, 1)
                    o = j.at(-3)
                    if k == 0 and o.inside:
                        for count in due(gate_steps, o.lin(GATE, 5)):
                            act.wait_ge(gate_steps, count)
                        act.activation(dif[0:HT], dif[0:HT], ACT.Exp).then_inc(gate_exponentials, 1)
                    b, kb = lag(j, k, 5)
                    if b.inside:
                        gather_heads(act, act.copy, b, kb, (2, 3), heads_gathered_by_scalar)
                    b, kb = lag(j, k, 1)
                    if b.inside:
                        for count in due(maxima_made, b.lin(BATS, kb + 1)):
                            act.wait_ge(maxima_made, count)
                        for t in range(UNITS[kb // G]):
                            mm = act.activation(s_sb[:, kb, t, :], s_sb[:, kb, t, :], ACT.Exp, bias=mx[:, kb, t:t + 1],
                                                accum_out=sm[:, kb, t:t + 1])
                        mm.then_inc(exponentials_made, 1)
                    b = j.at(-1)
                    if k == 4 and b.inside:
                        for count in due(heads_gathered_by_vector, j.lin(BATS)):
                            act.wait_ge(heads_gathered_by_vector, count)
                        for count in due(heads_gathered_by_scalar, j.lin(BATS)):
                            act.wait_ge(heads_gathered_by_scalar, count)
                        for count in due(attention_projected, b.lin(1)):
                            act.wait_ge(attention_projected, count)
                        act.copy(o_hl[0][:], oT[:, b.parity]).then_inc(heads_high, 1)

            run(act, body)
            for used in (scores_made, values_weighted, logits_kept, heads_gathered_by_vector, ln2_turned_kept, q_spread, ranks_made, gate_steps, logits_made):
                act.wait_ge(used, totals[id(used)])
            for p in range(2):
                act.wait_ge(x1_stored[p], totals[id(x1_stored[p])])
            for e in range(E):
                act.wait_ge(expert_weights_loaded[e % 4], 32 * (e // 4 + 1))
                act.copy(w_hi[:, e], staged(e)).then_inc(expert_weights_high, 1)
            act.wait_ge(table_steps, TAB_STEPS)

            def ffn(i):
                if i.inside:
                    for count in due(hidden_turned, i.lin(1, 1)):
                        act.wait_ge(hidden_turned, count)
                    for count in due(expert_out_made, i.lin(1, -1)):
                        act.wait_ge(expert_out_made, count)
                    act.copy(f_hh[:, i.parity], pf_t[i.parity][:]).then_inc(hidden_turned_high, 1)
                n = i.at(3)
                if n.inside:
                    for count in due(slots_turned, n.lin(1, 1)):
                        act.wait_ge(slots_turned, count)
                    for count in due(hidden_made, n.lin(1, -1)):
                        act.wait_ge(hidden_made, count)
                    act.copy(f_xh[:, n.parity], pf_x[n.parity][:]).then_inc(slots_turned_high, 1)
                n = i.at(1)
                if n.inside:
                    for count in due(hidden_biased, n.lin(1, 1)):
                        act.wait_ge(hidden_biased, count)
                    act.activation(f_h[:, n.parity, :], f_h[:, n.parity, :], ACT.Gelu).then_inc(gelu_made, 1)
                b = i.at(-1)
                if b.inside:
                    for count in due(expert_out_made, b.lin(1, 1)):
                        act.wait_ge(expert_out_made, count)
                    for count in due(slot_numbers_kept, b.lin(2, 2)):
                        act.wait_ge(slot_numbers_kept, count)
                    for count in due(expert_out_biased, b.lin(1, -1)):
                        act.wait_ge(expert_out_biased, count)
                    act.activation(f_t[:, b.parity, :], pf_y[b.parity][:], ACT.Copy, scale=f_cw[:, b.slot(4), :]).then_inc(expert_out_weighted, 1)

            run(act, ffn, **TILES)

        @block.gpsimd
        def _(pool):
            for count in due(weights_loaded, 16 * 19, pool):
                pool.wait_ge(weights_loaded, count)
            for count in due(buffers_cleared, 2, pool):
                pool.wait_ge(buffers_cleared, count)

            def body(j):
                for k in range(BATS):
                    b, kb = lag(j, k, 1)
                    if b.inside:
                        for count in due(sums_inverted, b.lin(BATS, kb + 1), pool):
                            pool.wait_ge(sums_inverted, count)
                        n = UNITS[kb // G]
                        pool.tensor_tensor(s_sb[:, kb, 0:n, :], s_sb[:, kb, 0:n, :],
                                           rs[:, kb, 0:n].unsqueeze(2).broadcast_to([P, n, KK]),
                                           ALU.mult).then_inc(probabilities_made, 1)
                    o, n1, n3 = j.at(-2), j.at(1), j.at(3)
                    if k == 1 and o.inside:
                        for count in due(ln2_variance, o.lin(1, 1), pool):
                            pool.wait_ge(ln2_variance, count)
                        for count in due(ln2_done, o.lin(2), pool):
                            pool.wait_ge(ln2_done, count)
                        pool.tensor_tensor(rs2[0:HT, :], ve2[0:HT, :], half_sb[0:HT, :], ALU.pow).then_inc(ln2_scale, 1)
                    b = j.at(-1)
                    if k == 0 and b.inside:
                        for count in due(residual_loaded[b.parity], b.turn(16, 16), pool):
                            pool.wait_ge(residual_loaded[b.parity], count)
                        pool.tensor_tensor(x_res[0:HT, b.parity], x_res[0:HT, b.parity],
                                           bo_sb[0:HT].broadcast_to([HT, 2, C]), ALU.add).then_inc(residual_biased, 1)
                    if k in (1, 2) and n1.inside:
                        g = k - 1
                        for count in due(q_kept, n1.lin(1, 1), pool):
                            pool.wait_ge(q_kept, count)
                        for count in due(scores_made, j.lin(BATS), pool):
                            pool.wait_ge(scores_made, count)
                        pool.tensor_tensor(
                            q_bd[:, n1.parity, g],
                            q_sb[:, n1.parity, g].rearrange("p (t q) -> p t q", t=NT).unsqueeze(2).broadcast_to([P, NT, HG, QQ]),
                            own_sb[:].unsqueeze(1).unsqueeze(3).broadcast_to([P, NT, HG, QQ]),
                            ALU.mult).then_inc(q_spread, 1)
                    if k == 4 and n3.inside:
                        for count in due(ln1_variance, n3.lin(1, 1), pool):
                            pool.wait_ge(ln1_variance, count)
                        for count in due(ln1_done, n3.lin(2), pool):
                            pool.wait_ge(ln1_done, count)
                        pool.tensor_tensor(rs1[0:HT, :], ve1[0:HT, :], half_sb[0:HT, :], ALU.pow).then_inc(ln1_scale, 1)
                    o = j.at(-3)
                    if k in (3, 4) and o.inside:
                        for count in due(gate_steps, o.lin(GATE, GATE), pool):
                            pool.wait_ge(gate_steps, count)
                        h = k - 3
                        for i in range(2):
                            pool.indirect_dma_start(
                                slots, bass.IndirectOffsetOnAxis(ap=pos[0:HT, o.parity, 2 * h + i:2 * h + i + 1], axis=0),
                                xn2[0:HT, o.parity, h, :], None).then_inc(tokens_dispatched[o.parity], 16)

            run(pool, body)
            for p in range(2):
                pool.wait_ge(x1_stored[p], totals[id(x1_stored[p])])
            for e in ON_POOL:
                pool.wait_ge(expert_weights_high, e + 1)
                pool.tensor_tensor(w_lo[:, e], staged(e), w_hi[:, e].bitcast(F32), ALU.subtract).then_inc(expert_weights_low_by_gpsimd, 1)
            pool.wait_ge(dummy_rows_stored, 16 * (2 + E))
            pool.wait_ge(table_steps, TAB_STEPS)

            begin, fetch, expert_of = experts(mybir.EngineType.Pool, 1, 1)

            def ffn(i):
                begin(i)
                n = i.at(1)
                if n.inside:
                    for count in due(slots_loaded[n.slot(4)], n.turn(16, 16, ring=4), pool):
                        pool.wait_ge(slots_loaded[n.slot(4)], count)
                    for count in due(expert_out_added, n.lin(16, -48), pool):
                        pool.wait_ge(expert_out_added, count)
                    mine = bass.AP(f_x[:].tensor, expert_of(n) + (n.slot(4) * ROW + C), [[4 * ROW, P], [1, 1]])
                    pool.tensor_copy(f_cw[:, n.slot(4), :], mine).then_inc(slot_numbers_kept, 1)
                    pool.tensor_copy(f_id[:, n.slot(4), :], f_x[:, n.slot(4), C + E:C + E + 1]).then_inc(slot_numbers_kept, 1)
                b = i.at(-1)
                if b.inside:
                    for count in due(expert_out_biased, b.lin(1, 1), pool):
                        pool.wait_ge(expert_out_biased, count)
                    for count in due(slot_numbers_kept, b.lin(2, 2), pool):
                        pool.wait_ge(slot_numbers_kept, count)
                    for count in due(expert_out_added, b.lin(16), pool):
                        pool.wait_ge(expert_out_added, count)
                    pool.indirect_dma_start(out, bass.IndirectOffsetOnAxis(ap=f_id[:, b.slot(4), :], axis=0),
                                            f_y[:, b.slot(4), :], None, compute_op=ALU.add).then_inc(expert_out_added, 16)

            run(pool, ffn, **TILES)


def kernel(**inputs):
    import numpy as _np
    import concourse.bacc as _bacc
    from concourse import mybir as _mybir
    from concourse.bass_utils import run_bass_kernel_spmd as _run

    nc = _bacc.Bacc("TRN2", target_bir_lowering=False, num_devices=1)
    d = {k.replace("L0_", ""): _np.asarray(v) for k, v in inputs.items()}
    qr, qc = _np.divmod(_np.arange(QQ), QS)
    kr, kc = _np.divmod(_np.arange(KK), KS)
    dr, dc = kr[None] - qr[:, None], kc[None] - qc[:, None]
    near = (dr >= 0) & (dr < WIN) & (dc >= 0) & (dc < WIN)
    mask = _np.tile(_np.where(near, 0.0, NEG).astype(_np.float32), (HEADS, 1)).reshape(P, KS, KS)
    own = _np.repeat(_np.eye(P * HEADS // d["x"].shape[-1], dtype=_np.float32), d["x"].shape[-1] // HEADS, axis=0)
    ntok, E = d["x"].size // d["x"].shape[-1], d["ffn_W1"].shape[0]
    dummy = _np.zeros((P, ROW), _np.float32)
    dummy[:, d["x"].shape[-1] + E] = ntok + _np.arange(P)
    ht = ROWS * d["x"].shape[2] // 2
    numbers = (_np.arange(P)[:, None] + ht * _np.arange(-2, 0)[None]).astype(_np.float32)
    named = {
        "x": d["x"], "wqT": d["conv_wq"].T, "wkT": d["conv_wk"].T, "wvT": d["conv_wv"].T, "woT": d["conv_wo"].T,
        "bq": d["conv_bq"].reshape(-1, P).T, "bk": d["conv_bk"].reshape(-1, P).T, "bv": d["conv_bv"], "bo": d["conv_bo"],
        "gate_w": d["ffn_gate_w"], "gate_b": d["ffn_gate_b"], "mask": mask, "own": own, "ident": _np.eye(P, dtype=_np.float32),
        "expert_no": _np.arange(E, dtype=_np.float32), "first_slot": _np.arange(E, dtype=_np.float32) * slots_of_expert(ntok),
        "dummy": dummy, "lower": _np.triu(_np.ones((P, P), _np.float32), 1), "numbers": numbers, "tile_no": _np.arange(tiles_in_all(ntok, E), dtype=_np.float32),
        "W1": d["ffn_W1"], "b1": d["ffn_b1"],
        "W2": d["ffn_W2"], "b2": d["ffn_b2"],
    }
    arrays, args = {}, []
    for name, a in named.items():
        a = _np.ascontiguousarray(a)
        arrays[f"in_{name}"] = a
        args.append(nc.dram_tensor(f"in_{name}", a.shape, _mybir.dt.from_np(a.dtype), kind="ExternalInput").ap())
    args.append(nc.dram_tensor("out_0", (ntok + P, d["x"].shape[-1]), _mybir.dt.float32, kind="ExternalOutput").ap())
    build(nc, *args)
    r = _run(nc, [arrays], core_ids=[0])
    return r.results[0]["out_0"][:ntok].reshape(d["x"].shape)
```
